# Optimizing a Trainium2 kernel written in Bass

```python
import numpy as np
import jax
import jax.numpy as jnp

def _softmax(x, axis=-1):
    return jax.nn.softmax(x, axis=axis)

def _gelu(x):
    return jax.nn.gelu(x, approximate=True)

def _silu(x):
    return jax.nn.silu(x)

def _sigmoid(x):
    return jax.nn.sigmoid(x)

def _layernorm(x, axis=-1, eps=1e-05):
    m = jnp.mean(x, axis=axis, keepdims=True)
    v = jnp.var(x, axis=axis, keepdims=True)
    return (x - m) / jnp.sqrt(v + eps)

def _scatter_add(tgt, idx, src, axis=0):
    return tgt.at[idx].add(src)

def _segment_sum(src, seg, n):
    return jax.ops.segment_sum(src, seg, n)
kernel_name = 'mk_flamingo_gated_d1_seqx_r4_699739'

def setup_inputs(seed: int=0):
    np.random.seed(seed)
    _w = jnp.asarray

    def _rec_inputs():
        import jax
        import jax.numpy as jnp
        _rk = jax.random.key(seed)
        x = 0.5 + 0.2887 * jax.random.normal(jax.random.fold_in(_rk, 1), (4, 512, 512), jnp.float32)
        _lenS = 512 - jax.random.randint(jax.random.fold_in(_rk, 7), (4,), 0, max(1, 512 // 4) + 1, jnp.int32)
        _lenS2 = 512 - jax.random.randint(jax.random.fold_in(_rk, 8), (4,), 0, max(1, 512 // 4) + 1, jnp.int32)
        _ctx_512P = jax.random.normal(jax.random.fold_in(_rk, 11), (4, 16, 128), jnp.float32)
        _ctx_512c = jax.random.dirichlet(jax.random.fold_in(_rk, 511), 0.3 * jnp.ones((16,), jnp.float32), (4, 512))
        _ctx_512t = jnp.einsum('bsk,bkd->bsd', _ctx_512c, _ctx_512P)
        _ctx_512t = _ctx_512t * jax.lax.rsqrt(jnp.mean(jnp.square(_ctx_512t)) + 1e-12) * 0.953939
        ctx_512 = 7.22013e-05 + 1.00017 * (_ctx_512t + 0.3 * jax.random.normal(jax.random.fold_in(_rk, 611), (4, 512, 128), jnp.float32))
        _validS = jnp.arange(512)[None, :] < _lenS[:, None]
        _validS2 = jnp.arange(512)[None, :] < _lenS2[:, None]
        _causal = jnp.tril(jnp.ones((512, 512), dtype=bool))
        mask_SxS2_bk1 = jnp.broadcast_to(_validS2[0:1, :], (512, 512))
        mask_BxS2_bf0 = jnp.logical_not(jnp.ones((4, 512), dtype=bool))
        _g = jax.random.normal(jax.random.fold_in(_rk, 9001), (2, 1), jnp.float32)
        _g = jnp.sign(_g) * jnp.maximum(jnp.abs(_g), 1.0) + (_g == 0) * 1.0
        g_xattn = _g[0]
        g_ffn = _g[1]
        return (x, ctx_512, mask_SxS2_bk1, mask_BxS2_bf0, g_xattn, g_ffn)
    x, ctx_512, mask_SxS2_bk1, mask_BxS2_bf0, g_xattn, g_ffn = _rec_inputs()

    def _L0_xattn_setup():
        import jax, jax.numpy as jnp
        import numpy as np
        B, S, H = (8, 512, 128)
        key = jax.random.key(seed)
        kq, kk, kqc, kwq, kwk = jax.random.split(key, 5)
        q = jax.random.normal(kq, (B, S, H), dtype=jnp.float32)
        k = jax.random.normal(kk, (B, S, H), dtype=jnp.float32)
        qc_score = jax.random.uniform(kqc, (B, S, S), dtype=jnp.float32)
        attn_mask = jnp.triu(jnp.ones((S, S), dtype=bool), k=1)
        key_padding_mask = jnp.zeros((B, S), dtype=bool)
        scale = 1.0 / np.sqrt(H)
        Wq = jax.random.normal(kwq, (H, H), dtype=jnp.float32) * scale
        Wk = jax.random.normal(kwk, (H, H), dtype=jnp.float32) * scale
        bq = jnp.zeros((H,), dtype=jnp.float32)
        bk = jnp.zeros((H,), dtype=jnp.float32)
        return {'q': q, 'k': k, 'attn_mask': attn_mask, 'key_padding_mask': key_padding_mask, 'qc_score': qc_score, 'Wq': Wq, 'bq': bq, 'Wk': Wk, 'bk': bk}
    _L0_xattn_all = _L0_xattn_setup()
    _L0_xattn_in = {k: v for k, v in _L0_xattn_all.items() if k in ('Wq', 'bq', 'Wk', 'bk')}
    del _L0_xattn_all

    def _L0_ffn_setup():
        import jax, jax.numpy as jnp
        import numpy as np
        B, S, D = (4, 512, 512)
        E, K, M = (8, 2, 256)
        key = jax.random.key(seed)
        k0, k1, k2, k3, k4 = jax.random.split(key, 5)
        d_scale = D ** (-0.5)
        m_scale = M ** (-0.5)
        return {'x': jax.random.normal(k0, (B, S, D), jnp.float32), 'w_gate': jax.random.normal(k1, (D, E), jnp.float32) * d_scale, 'wi_0': jax.random.normal(k2, (E, D, M), jnp.float32) * d_scale, 'wi_1': jax.random.normal(k3, (E, D, M), jnp.float32) * d_scale, 'wo': jax.random.normal(k4, (E, M, D), jnp.float32) * m_scale}
    _L0_ffn_all = _L0_ffn_setup()
    _L0_ffn_in = {k: v for k, v in _L0_ffn_all.items() if k in ('w_gate', 'wi_0', 'wi_1', 'wo')}
    del _L0_ffn_all
    return {'x': x, 'ctx_512': ctx_512, 'mask_SxS2_bk1': mask_SxS2_bk1, 'mask_BxS2_bf0': mask_BxS2_bf0, 'g_xattn': g_xattn, 'g_ffn': g_ffn, 'L0_xattn_Wq': _L0_xattn_in['Wq'], 'L0_xattn_bq': _L0_xattn_in['bq'], 'L0_xattn_Wk': _L0_xattn_in['Wk'], 'L0_xattn_bk': _L0_xattn_in['bk'], 'L0_ffn_w_gate': _L0_ffn_in['w_gate'], 'L0_ffn_wi_0': _L0_ffn_in['wi_0'], 'L0_ffn_wi_1': _L0_ffn_in['wi_1'], 'L0_ffn_wo': _L0_ffn_in['wo']}

def reference(x, ctx_512, mask_SxS2_bk1, mask_BxS2_bf0, g_xattn, g_ffn, L0_xattn_Wq, L0_xattn_bq, L0_xattn_Wk, L0_xattn_bk, L0_ffn_w_gate, L0_ffn_wi_0, L0_ffn_wi_1, L0_ffn_wo):
    import jax
    import jax.numpy as jnp

    def _L0_xattn_ref(q, k, attn_mask, key_padding_mask, qc_score, Wq, bq, Wk, bk):
        import jax, jax.numpy as jnp
        import numpy as np
        B, S, H = (8, 512, 128)
        qp = jnp.einsum('bsh,oh->bso', q, Wq) + bq
        kp = jnp.einsum('bth,oh->bto', k, Wk) + bk
        scaling = jnp.asarray(float(H) ** (-0.5), dtype=qp.dtype)
        scores = jnp.einsum('bsh,bth->bst', qp, kp) * scaling
        scores = scores * qc_score
        mask = attn_mask[None, :, :] | key_padding_mask[:, None, :]
        scores = jnp.where(mask, -jnp.inf, scores)
        return jax.nn.softmax(scores, axis=-1)

    def _L0_ffn_ref(x, w_gate, wi_0, wi_1, wo):
        import jax, jax.numpy as jnp
        import numpy as np
        B, S, D = (4, 512, 512)
        E, K, M = (8, 2, 256)
        b, s, d = x.shape
        e = w_gate.shape[1]
        xf = x.reshape(-1, d)
        logits = jnp.dot(xf, w_gate)
        top_logits, top_idx = jax.lax.top_k(logits, K)
        weights = jax.nn.softmax(top_logits, axis=-1)
        flat_idx = top_idx.reshape(-1)
        sort_order = jnp.argsort(flat_idx)
        token_ids = sort_order // K
        sorted_x = jnp.take(xf, token_ids, axis=0)
        group_sizes = jnp.bincount(flat_idx, length=E).astype(jnp.int32)
        h0 = jax.lax.ragged_dot(sorted_x, wi_0, group_sizes)
        h1 = jax.lax.ragged_dot(sorted_x, wi_1, group_sizes)
        inter = jax.nn.silu(h0) * h1
        out_sorted = jax.lax.ragged_dot(inter, wo, group_sizes)
        unsort = jnp.argsort(sort_order)
        out = jnp.take(out_sorted, unsort, axis=0).reshape(-1, K, d)
        out = jnp.einsum('tkd,tk->td', out, weights)
        return out.reshape(b, s, d)
    x = x + jnp.tanh(g_xattn[0]) * _L0_xattn_ref(ctx_512, ctx_512, mask_SxS2_bk1, mask_BxS2_bf0, _layernorm(x, axis=-1), L0_xattn_Wq, L0_xattn_bq, L0_xattn_Wk, L0_xattn_bk)
    x = x + jnp.tanh(g_ffn[0]) * _L0_ffn_ref(_layernorm(x, axis=-1), L0_ffn_w_gate, L0_ffn_wi_0, L0_ffn_wi_1, L0_ffn_wo)
    return x

_drawn_inputs = setup_inputs


def setup_inputs(seed=0):
    import zlib

    import numpy as np

    out = dict(_drawn_inputs(seed))
    spreads = {'L0_xattn_bq': (0.0, 0.1), 'L0_xattn_bk': (0.0, 0.359)}
    factors = {}
    for name, (base, spread) in spreads.items():
        noise = np.random.default_rng([zlib.crc32(name.encode()), seed]).standard_normal(out[name].shape)
        drawn = base * np.exp(spread * noise) if base else spread * noise
        out[name] = jnp.asarray(drawn.astype(out[name].dtype))
    for name, factor in factors.items():
        out[name] = (out[name] * factor).astype(out[name].dtype)
    return out
```

```python
from contextlib import ExitStack

import concourse.bass as bass
from concourse import mybir

F32 = mybir.dt.float32
BF16 = mybir.dt.bfloat16
I32 = mybir.dt.int32
U8 = mybir.dt.uint8
ALU = mybir.AluOpType
ACT = mybir.ActivationFunctionType
AX_X = mybir.AxisListType.X

P = 128
MASKED = -1e30
ALL_MASKED = -5e29
FAR = 65536.0
EPS = 1e-5
TOP_K = 2
ROW_BUFS = 4


def dims(x, ctx, w_gate, wi_0):
    B, S, D = x.shape
    E, M = w_gate.shape[1], wi_0.shape[2]
    tokens = B * S
    return dict(
        B=B, S=S, D=D, H=ctx.shape[2], E=E, M=M, tokens=tokens, KT=S // P, NT=tokens // P,
        DC=D // P, MC=M // P, ROW=D + E,
        TILES=(TOP_K * tokens + E * (P - 1)) // P,
    )


def gated_attention_moe(nc, x, ctx_in, mask_st, mask_bt, g_attn, g_ffn, wq, bq, wk, bk,
                        w_gate, wi_0, wi_1, wo, out, rows):
    n = dims(x, ctx_in, w_gate, wi_0)
    B, S, D, H, E, M = (n[k] for k in ("B", "S", "D", "H", "E", "M"))
    tokens, KT, NT, DC, MC, ROW, TILES = (n[k] for k in ("tokens", "KT", "NT", "DC", "MC", "ROW", "TILES"))
    scale = float(H) ** -0.5
    PAIRS = TOP_K * NT
    LOOPS = (TILES - 3) // ROW_BUFS
    assert H == P and D == 512 and M == 256 and 1 + LOOPS * ROW_BUFS + 2 == TILES

    with ExitStack() as ctx:
        def sb(name, shape, dt=F32):
            return ctx.enter_context(nc.sbuf_tensor(name, shape, dt))

        def sem(name):
            return ctx.enter_context(nc.semaphore(name))

        bank = [ctx.enter_context(nc.psum_tensor(f"bank{i}", [P, 512], F32)) for i in range(8)]

        ident = sb("ident", [P, P])
        upper = sb("upper", [P, P], BF16)
        ones = sb("ones", [P, P], BF16)
        lane_row = sb("lane_row", [P, P])
        tile_row = sb("tile_row", [P, TILES])
        expert_m = sb("expert_m", [P, E])
        step_row = sb("step_row", [P, NT])
        token_rel = sb("token_rel", [P, TOP_K, NT])
        pad_row = sb("pad_row", [P, 1])
        zero_rows = sb("zero_rows", [P, ROW])
        eps_col = sb("eps_col", [P, 1])
        wqk = sb("wqk", [P, 2, P])
        wqkT = sb("wqkT", [P, 2, P])
        bqk = sb("bqk", [P, 2])
        gates = sb("gates", [P, 2])
        tgates = sb("tgates", [P, 2])
        wg_sb = sb("wg_sb", [P, DC, E])
        wi_sb = sb("wi_sb", [P, E, DC, 2 * M])
        wo_sb = sb("wo_sb", [P, E, MC, D])
        m8 = sb("m8", [P, KT, S], U8)
        kp8 = sb("kp8", [P, B, S], U8)
        mask_s = sb("mask_s", [P, KT, S])
        mask_b = sb("mask_b", [P, 2, S])
        mask_f = sb("mask_f", [P, 4, S])
        x_sb = sb("x_sb", [P, 2, KT, S])
        c_sb = sb("c_sb", [P, 2, KT, P])
        cT = sb("cT", [P, S])
        qkT = sb("qkT", [P, 2, 2, S])
        prob = sb("prob", [P, 2, KT, S])
        xn = sb("xn", [P, 2, KT, D])
        xnT = sb("xnT", [P, 2, DC, P])
        stats = sb("stats", [P, 2, KT, 6])
        mv = sb("mv", [P, 2, 2, KT, 2])
        lnv = sb("lnv", [P, 2, KT])
        rstd0 = sb("rstd0", [P, 2, KT])
        tmp = sb("tmp", [P, 2, KT])
        rstd = sb("rstd", [P, 2, 2, KT])
        shift = sb("shift", [P, 2, KT])
        smax = sb("smax", [P, 2, KT])
        esc = sb("esc", [P, 2, KT])
        ebi = sb("ebi", [P, 2, KT])
        esum = sb("esum", [P, 2, KT])
        live = sb("live", [P, KT])
        coef = sb("coef", [P, KT])
        logit = sb("logit", [P, KT, E])
        cand = sb("cand", [P, KT, E])
        eq = sb("eq", [P, KT, E])
        best = sb("best", [P, 2, KT])
        which = sb("which", [P, KT])
        gap = sb("gap", [P, KT])
        egap = sb("egap", [P, KT])
        share = sb("share", [P, 2, KT])
        wtok = sb("wtok", [P, 2, KT, E])
        chose = sb("chose", [P, TOP_K, NT, E])
        chosen = sb("chosen", [P, E, NT], BF16)
        total = sb("total", [P, E, NT])
        incl = sb("incl", [P, E * NT])
        count = sb("count", [P, E])
        cmp_c = sb("cmp_c", [P, E, NT])
        ntile = sb("ntile", [P, E])
        tend = sb("tend", [P, E])
        adj = sb("adj", [P, E])
        place = sb("place", [P, E, NT])
        pick = sb("pick", [P, TOP_K, NT, E])
        pos = sb("pos", [P, PAIRS])
        pos_i = sb("pos_i", [P, PAIRS], I32)
        hi_i = sb("hi_i", [P, PAIRS], I32)
        hi = sb("hi", [P, PAIRS])
        lo = sb("lo", [P, PAIRS])
        val = sb("val", [P, PAIRS])
        at_lane = sb("at_lane", [P, 4, P])
        at_tile = sb("at_tile", [P, 4, TILES])
        slot_row = sb("slot_row", [P, TILES], I32)
        cmp_t = sb("cmp_t", [P, TILES, E])
        eid = sb("eid", [P, TILES])
        eid_i = sb("eid_i", [P, TILES], I32)
        is_exp = sb("is_exp", [P, TILES, E])
        gidx = sb("gidx", [P, ROW_BUFS], I32)
        sidx = sb("sidx", [P, 2], I32)
        xg = xn[:, :, :, :].rearrange("p a k d -> p (a k d)")[:, 0:ROW_BUFS * ROW]\
            .rearrange("p (q n) -> p q n", q=ROW_BUFS)
        old_prob = prob[:, :, :, :].rearrange("p a k d -> p (a k d)")

        def reuse(start, width):
            return old_prob[:, start:start + 2 * width].rearrange("p (a n) -> p a n", a=2)

        xgT = reuse(0, D)
        y_sb = reuse(2 * D, D)
        gate = reuse(4 * D, M)
        inter = reuse(4 * D + 2 * M, M)
        interT = reuse(4 * D + 4 * M, M)
        wdump = sb("wdump", [P, 2, E])
        wslot = sb("wslot", [P, 2])

        ps_score = bank[0:3]
        ps_logit = bank[3]
        ps_cT = bank[4]
        ps_q, ps_k = bank[5], bank[4]
        ps_xT = bank[6:8]
        ps_within, ps_total, ps_slot = bank[0], bank[1], bank[2]
        ps_h, ps_gT, ps_iT, ps_y = bank[0:2], bank[2:4], bank[4:6], bank[6:8]

        s_w = sem("small_weights_loaded")
        s_mask = sem("masks_loaded")
        s_x = [sem(f"x_loaded_{b}") for b in range(B)]
        s_c = [sem(f"ctx_loaded_{b}") for b in range(B)]
        s_big = sem("expert_weights_loaded")
        s_const = sem("constants_made")
        s_pool = sem("pool_step")
        s_tg = sem("gates_squashed")
        s_wT = sem("wqk_transposed")
        s_wTc = sem("wqk_copied")
        s_cT = sem("ctx_transposed")
        s_cTc = sem("ctx_copied")
        s_q = sem("q_projected")
        s_k = sem("k_projected")
        s_qc = sem("q_biased")
        s_kc = sem("k_biased")
        s_sc = sem("scores_made")
        s_t1 = sem("scores_taken")
        s_mf = sem("mask_tile_made")
        s_t2 = sem("mask_tile_used")
        s_dve = sem("dve_step")
        s_var = sem("variance_ready")
        s_r0 = sem("rstd_guess")
        s_act = sem("act_step")
        s_aff = sem("exp_operands_ready")
        s_e = sem("exp_done")
        s_x1 = sem("x1_done")
        s_sh = sem("norm_operands_ready")
        s_xn = sem("xn_done")
        s_xT = sem("xn_transposed")
        s_xTc = sem("xnT_copied")
        s_lg = sem("logits_made")
        s_lgc = sem("logits_taken")
        s_gap = sem("gap_ready")
        s_egap = sem("gap_exp")
        s_wt = sem("token_weights_ready")
        s_x1st = [sem(f"x1_stored_{i}") for i in range(2)]
        s_xnst = [sem(f"xn_stored_{i}") for i in range(2)]
        s_wst = [sem(f"token_weights_stored_{i}") for i in range(2)]
        s_zst = sem("padding_stored")
        s_ch = sem("chosen_ready")
        s_rank = sem("ranks_made")
        s_oh = sem("pair_onehots")
        s_sl = sem("pair_summed")
        s_slot = sem("slot_rows_ready")
        s_eid = sem("tile_experts_ready")
        s_g = [sem(f"rows_gathered_{i}") for i in range(ROW_BUFS)]
        s_gT = sem("rows_transposed")
        s_gTc = sem("rowsT_copied")
        s_h = sem("hidden_made")
        s_gate = sem("gate_done")
        s_ws = sem("slot_weight_ready")
        s_in = sem("inter_done")
        s_iT = sem("inter_transposed")
        s_iTc = sem("interT_copied")
        s_y = sem("y_made")
        s_yc = sem("y_copied")
        s_sct = sem("y_scattered")
        s_gi = sem("gather_index_ready")
        s_si = sem("scatter_index_ready")
        s_pass = sem("waits_passed")

        block = ctx.enter_context(nc.Block())

        out_v = out[0:tokens, :].rearrange("(b k p) d -> b p k d", b=B, p=P)
        xn_v = rows[0:tokens, 0:D].rearrange("(b k p) d -> b p k d", b=B, p=P)
        wt_v = rows[0:tokens, D:ROW].rearrange("(b k p) d -> b p k d", b=B, p=P)

        @block.sync
        def _(sp):
            sp.dma_start(wqk[:, 0, :], wq).then_inc(s_w, 16)
            sp.dma_start(wqk[:, 1, :], wk).then_inc(s_w, 16)
            sp.dma_start(bqk[:, 0:1], bq.rearrange("(o a) -> o a", a=1)).then_inc(s_w, 16)
            sp.dma_start(bqk[:, 1:2], bk.rearrange("(o a) -> o a", a=1)).then_inc(s_w, 16)
            sp.dma_start(gates[:, 0:1], g_attn.partition_broadcast(P)).then_inc(s_w, 16)
            sp.dma_start(gates[:, 1:2], g_ffn.partition_broadcast(P)).then_inc(s_w, 16)

            def load_batch(b):
                if b >= 2:
                    sp.wait_ge(s_cT, b - 1)
                sp.dma_start(c_sb[:, b % 2], ctx_in[b].rearrange("(k p) h -> p k h", p=P)).then_inc(s_c[b], 16)
                if b >= 2:
                    sp.wait_ge(s_x1st[b % 2], 16 * (b // 2))
                    sp.wait_ge(s_xn, KT * (b - 1))
                sp.dma_start(x_sb[:, b % 2], x[b].rearrange("(k p) d -> p k d", p=P)).then_inc(s_x[b], 16)

            load_batch(0)
            sp.dma_start(m8[:, :, :], mask_st.rearrange("(k p) t -> p k t", p=P)).then_inc(s_mask, 16)
            sp.dma_start(kp8[:, :, :], mask_bt.partition_broadcast(P)).then_inc(s_mask, 16)
            sp.dma_start(wg_sb[:, :, :], w_gate.rearrange("(c p) e -> p c e", p=P)).then_inc(s_w, 16)
            load_batch(1)

            def load_expert(e):
                sp.dma_start(wi_sb[:, e, :, 0:M], wi_0[e].rearrange("(c p) m -> p c m", p=P)).then_inc(s_big, 16)
                sp.dma_start(wi_sb[:, e, :, M:2 * M], wi_1[e].rearrange("(c p) m -> p c m", p=P)).then_inc(s_big, 16)
                sp.dma_start(wo_sb[:, e, :, :], wo[e].rearrange("(c p) d -> p c d", p=P)).then_inc(s_big, 16)

            for e in range(0, 2):
                load_expert(e)
            load_batch(2)
            for e in range(2, 4):
                load_expert(e)
            load_batch(3)
            for e in range(4, E):
                load_expert(e)

        @block.gpsimd
        def _(pool):
            step = [0]

            def link(ins):
                step[0] += 1
                ins.then_inc(s_pool, 1)
                pool.wait_ge(s_pool, step[0])

            link(pool.memset(ident[:, :], 0.0))
            pool.affine_select(out=ident[:, :], in_=ident[:, :], compare_op=ALU.not_equal, fill=1.0, base=0,
                               pattern=[[-1, P]], channel_multiplier=1).then_inc(s_const, 1)
            pool.memset(eps_col[:, :], EPS).then_inc(s_const, 1)
            pool.wait_ge(s_mask, 32)
            link(pool.tensor_scalar(mask_s[:, :, :], m8[:, :, :], MASKED, None, ALU.mult))
            for b in range(B):
                if b >= 2:
                    pool.wait_ge(s_mf, KT * (b - 1))
                link(pool.tensor_scalar(mask_b[:, b % 2, :], kp8[:, b, :], MASKED, None, ALU.mult))
                for k in range(KT):
                    i = b * KT + k
                    if i >= 4:
                        pool.wait_ge(s_t2, i - 3)
                    pool.tensor_tensor(mask_f[:, i % 4, :], mask_s[:, k, :], mask_b[:, b % 2, :],
                                       ALU.add).then_inc(s_mf, 1)
                if b == 0:
                    pool.iota(expert_m[:, :], [[1, E]], base=-E, channel_multiplier=0,
                              allow_small_or_imprecise_dtypes=True).then_inc(s_const, 1)
                    link(pool.memset(upper[:, :], 1.0))
                    link(pool.affine_select(out=upper[:, :], in_=upper[:, :], compare_op=ALU.is_gt, fill=0.0,
                                            base=0, pattern=[[1, P]], channel_multiplier=-1))
                    pool.memset(ones[:, :], 1.0)
                    for t, pattern, base, mult in (
                        (lane_row, [[1, P]], 0, 0), (tile_row, [[1, TILES]], 0, 0), (step_row, [[P, NT]], 0, 0),
                        (token_rel, [[0, TOP_K], [P, NT]], -tokens, 1), (pad_row, [[0, 1]], tokens, 1),
                    ):
                        pool.iota(t[:], pattern, base=base, channel_multiplier=mult,
                                  allow_small_or_imprecise_dtypes=True)
                    link(pool.memset(zero_rows[:, :], 0.0))
                    pool.dma_start(rows[tokens:tokens + P, :], zero_rows[:, :]).then_inc(s_zst, 16)
                    pool.dma_start(out[tokens:tokens + P, :], zero_rows[:, 0:D]).then_inc(s_zst, 16)
                    pool.memset(pos_i[:, :], 0).then_inc(s_const, 1)

            pool.wait_ge(s_slot, 1)
            pool.wait_ge(s_zst, 32)
            for i in range(2):
                pool.wait_ge(s_xnst[i], 16 * (B // 2))
                pool.wait_ge(s_wst[i], 16 * (B // 2))
                pool.wait_ge(s_x1st[i], 16 * (B // 2))

            def waited():
                pool.sem_inc(s_pass, 1)

            def gather(kk, r):
                q = r % ROW_BUFS
                pool.tensor_copy(gidx[:, q:q + 1], slot_row[:, bass.ds(ROW_BUFS * kk + r, 1)]).then_inc(s_gi, 1)
                pool.wait_ge(s_gi, ROW_BUFS * kk + r + 1)
                waited()
                pool.indirect_dma_start(xg[:, q, :], None, rows,
                                        bass.IndirectOffsetOnAxis(ap=gidx[:, q:q + 1], axis=0)).then_inc(s_g[q], 16)

            def scatter(kk, r):
                q = r % 2
                pool.tensor_copy(sidx[:, q:q + 1], slot_row[:, bass.ds(ROW_BUFS * kk + r, 1)]).then_inc(s_si, 1)
                pool.wait_ge(s_si, ROW_BUFS * kk + r + 1)
                pool.wait_ge(s_yc, ROW_BUFS * kk + r + 1)
                waited()
                pool.indirect_dma_start(out, bass.IndirectOffsetOnAxis(ap=sidx[:, q:q + 1], axis=0), y_sb[:, q, :],
                                        None, compute_op=ALU.add).then_inc(s_sct, 16)
                pool.wait_ge(s_sct, 16 * (ROW_BUFS * kk + r + 1))

            for r in range(ROW_BUFS):
                gather(0, r)
            turns = (TILES - ROW_BUFS) // ROW_BUFS
            with pool.Fori(0, turns) as kk:
                for r in range(ROW_BUFS):
                    scatter(kk, r)
                    gather(kk, r + ROW_BUFS)
            for j in range(turns * ROW_BUFS, TILES):
                scatter(0, j)
                if j + ROW_BUFS < TILES:
                    gather(0, j + ROW_BUFS)

        @block.scalar
        def _(act):
            step = [0]

            def link(ins):
                step[0] += 1
                ins.then_inc(s_act, 1)
                act.wait_ge(s_act, step[0])

            act.wait_ge(s_w, 16 * 7)
            act.activation(tgates[:, :], gates[:, :], ACT.Tanh).then_inc(s_tg, 1)
            act.wait_ge(s_const, 2)

            def guess(norm, b, nth):
                act.wait_ge(s_var, nth)
                link(act.activation(lnv[:, norm, :], mv[:, norm, b % 2, :, 1], ACT.Ln, bias=eps_col[:, 0:1]))
                act.activation(rstd0[:, norm, :], lnv[:, norm, :], ACT.Exp, scale=-0.5).then_inc(s_r0, 1)

            def project_out(b):
                act.wait_ge(s_cT, b + 1)
                if b >= 1:
                    act.wait_ge(s_k, b)
                act.activation(cT[:, :], ps_cT[:, :], ACT.Copy).then_inc(s_cTc, 1)
                if b >= 2:
                    act.wait_ge(s_sc, KT * (b - 1))
                act.wait_ge(s_q, b + 1)
                act.activation(qkT[:, b % 2, 0, :], ps_q[:, :], ACT.Identity, bias=bqk[:, 0:1]).then_inc(s_qc, 1)
                act.wait_ge(s_k, b + 1)
                act.activation(qkT[:, b % 2, 1, :], ps_k[:, :], ACT.Identity, bias=bqk[:, 1:2]).then_inc(s_kc, 1)

            def exps(b):
                for k in range(KT):
                    act.wait_ge(s_aff, KT * b + k + 1)
                    act.activation(prob[:, b % 2, k, :], prob[:, b % 2, k, :], ACT.Exp, scale=esc[:, b % 2, k:k + 1],
                                   bias=ebi[:, b % 2, k:k + 1], accum_out=esum[:, b % 2, k:k + 1]).then_inc(s_e, 1)

            def norm_out(b):
                act.wait_ge(s_x1, KT * (b + 1))
                act.dma_start(out_v[b], x_sb[:, b % 2]).then_inc(s_x1st[b % 2], 16)
                act.wait_ge(s_sh, b + 1)
                for k in range(KT):
                    if b >= 2 and k == 0:
                        act.wait_ge(s_xnst[b % 2], 16 * (b // 2))
                        act.wait_ge(s_xT, KT * (b - 1))
                    act.activation(xn[:, b % 2, k, :], x_sb[:, b % 2, k, :], ACT.Identity,
                                   scale=rstd[:, 1, b % 2, k:k + 1], bias=shift[:, b % 2, k:k + 1]).then_inc(s_xn, 1)
                for k in range(KT):
                    i = KT * b + k
                    act.wait_ge(s_xT, i + 1)
                    if i >= 2:
                        act.wait_ge(s_lg, i - 1)
                    act.activation(xnT[:, i % 2].rearrange("p c t -> p (c t)"), ps_xT[i % 2][:, :],
                                   ACT.Copy).then_inc(s_xTc, 1)
                    if k == 0:
                        act.wait_ge(s_xn, KT * (b + 1))
                        act.dma_start(xn_v[b], xn[:, b % 2]).then_inc(s_xnst[b % 2], 16)

            def top2_exp(b):
                act.wait_ge(s_gap, b + 1)
                act.activation(egap[:, :], gap[:, :], ACT.Exp).then_inc(s_egap, 1)
                act.wait_ge(s_wt, b + 1)
                act.dma_start(wt_v[b], wtok[:, b % 2]).then_inc(s_wst[b % 2], 16)

            guess(0, 0, 1)
            project_out(0)
            for b in range(B):
                if b + 1 < B:
                    guess(0, b + 1, 2 * b + 2)
                exps(b)
                if b + 1 < B:
                    project_out(b + 1)
                guess(1, b, 2 * b + 2 + (b + 1 < B))
                norm_out(b)
                top2_exp(b)

            def rows_out(kk, r):
                j = ROW_BUFS * kk + r
                act.wait_ge(s_gT, j + 1)
                if r >= 2:
                    act.wait_ge(s_h, j - 1)
                act.activation(xgT[:, r % 2, :], ps_gT[r % 2][:, :], ACT.Copy).then_inc(s_gTc, 1)

            def silu(kk, r):
                j = ROW_BUFS * kk + r
                act.wait_ge(s_h, j + 1)
                if r >= 2:
                    act.wait_ge(s_in, j - 1)
                act.activation(gate[:, r % 2, :], ps_h[r % 2][:, 0:M], ACT.Silu).then_inc(s_gate, 1)

            rows_out(0, 0)
            rows_out(0, 1)
            silu(0, 0)
            silu(0, 1)
            with act.Fori(0, LOOPS) as kk:
                for r in range(2, 2 + ROW_BUFS):
                    rows_out(kk, r)
                    silu(kk, r)
            rows_out(0, TILES - 1)
            silu(0, TILES - 1)

        @block.tensor
        def _(pe):
            pe.wait_ge(s_w, 16 * 7)
            pe.wait_ge(s_const, 1)
            for i in range(2):
                last = pe.transpose(ps_xT[0][:, i * P:(i + 1) * P], wqk[:, i, :], ident[:, :])
            last.then_inc(s_wT, 1)

            def project(b):
                pe.wait_ge(s_c[b], 16)
                if b >= 1:
                    pe.wait_ge(s_kc, b)
                for k in range(KT):
                    last = pe.transpose(ps_cT[:, k * P:(k + 1) * P], c_sb[:, b % 2, k, :], ident[:, :])
                last.then_inc(s_cT, 1)
                pe.wait_ge(s_cTc, b + 1)
                if b == 0:
                    pe.wait_ge(s_wTc, 1)
                if b >= 1:
                    pe.wait_ge(s_qc, b)
                pe.matmul(ps_q[:, :], wqkT[:, 0, :], cT[:, :], start=True, stop=True).then_inc(s_q, 1)
                pe.matmul(ps_k[:, :], wqkT[:, 1, :], cT[:, :], start=True, stop=True).then_inc(s_k, 1)

            def scores(b):
                pe.wait_ge(s_qc, b + 1)
                pe.wait_ge(s_kc, b + 1)
                for k in range(KT):
                    i = KT * b + k
                    if i >= 3:
                        pe.wait_ge(s_t1, i - 2)
                    pe.matmul(ps_score[i % 3][:, :], qkT[:, b % 2, 0, k * P:(k + 1) * P], qkT[:, b % 2, 1, :],
                              start=True, stop=True).then_inc(s_sc, 1)

            def turn(b, k):
                i = KT * b + k
                pe.wait_ge(s_xn, i + 1)
                if i >= 2:
                    pe.wait_ge(s_xTc, i - 1)
                elif i == 0:
                    pe.wait_ge(s_wTc, 1)
                for c in range(DC):
                    last = pe.transpose(ps_xT[i % 2][:, c * P:(c + 1) * P], xn[:, b % 2, k, c * P:(c + 1) * P],
                                        ident[:, :])
                last.then_inc(s_xT, 1)

            def route(b, k):
                i = KT * b + k
                pe.wait_ge(s_xTc, i + 1)
                if k == 0 and b >= 1:
                    pe.wait_ge(s_lgc, b)
                for c in range(DC):
                    last = pe.matmul(ps_logit[:, k * E:(k + 1) * E], xnT[:, i % 2, c, :], wg_sb[:, c, :],
                                     start=(c == 0), stop=(c == DC - 1))
                last.then_inc(s_lg, 1)

            project(0)
            scores(0)
            for b in range(B):
                if b + 1 < B:
                    project(b + 1)
                turn(b, 0)
                for k in range(1, KT):
                    turn(b, k)
                    route(b, k - 1)
                route(b, KT - 1)
                if b + 1 < B:
                    scores(b + 1)

            pe.wait_ge(s_const, 4)
            pe.wait_ge(s_ch, 1)
            ch = chosen[:, :, :].rearrange("p e i -> p (e i)")
            pe.matmul(ps_total[:, 0:E * NT], ones[:, :], ch, start=True, stop=True)
            pe.matmul(ps_within[:, 0:E * NT], upper[:, :], ch, start=True, stop=True).then_inc(s_rank, 1)
            for j in range(PAIRS):
                pe.wait_ge(s_oh, j + 1)
                pe.matmul(ps_slot[:, 0:TILES], at_lane[:, j % 4, :], at_tile[:, j % 4, :],
                          start=(j == 0), stop=(j == PAIRS - 1)).then_inc(s_sl, 1)

            def rows_turn(kk, r):
                j = ROW_BUFS * kk + r
                pe.wait_ge(s_g[r % ROW_BUFS], 16 * (kk + r // ROW_BUFS + 1))
                if r >= 2:
                    pe.wait_ge(s_gTc, j - 1)
                for c in range(DC):
                    last = pe.transpose(ps_gT[r % 2][:, c * P:(c + 1) * P],
                                        xg[:, r % ROW_BUFS, c * P:(c + 1) * P], ident[:, :])
                last.then_inc(s_gT, 1)

            def expert(kk, r):
                return pe.value_load(eid_i[0:1, bass.ds(ROW_BUFS * kk + r, 1)], min_val=0, max_val=E - 1)

            def hidden(kk, r, e):
                j = ROW_BUFS * kk + r
                pe.wait_ge(s_gTc, j + 1)
                if r >= 2:
                    pe.wait_ge(s_in, j - 1)
                for c in range(DC):
                    last = pe.matmul(ps_h[r % 2][:, :], xgT[:, r % 2, c * P:(c + 1) * P],
                                     wi_sb[:, bass.ds(e, 1), c, :], start=(c == 0), stop=(c == DC - 1))
                last.then_inc(s_h, 1)

            def inter_turn(kk, r):
                j = ROW_BUFS * kk + r
                pe.wait_ge(s_in, j + 1)
                if r >= 2:
                    pe.wait_ge(s_iTc, j - 1)
                for c in range(MC):
                    last = pe.transpose(ps_iT[r % 2][:, c * P:(c + 1) * P], inter[:, r % 2, c * P:(c + 1) * P],
                                        ident[:, :])
                last.then_inc(s_iT, 1)

            def down(kk, r, e):
                j = ROW_BUFS * kk + r
                pe.wait_ge(s_iTc, j + 1)
                if r >= 2:
                    pe.wait_ge(s_yc, j - 1)
                for c in range(MC):
                    last = pe.matmul(ps_y[r % 2][:, :], interT[:, r % 2, c * P:(c + 1) * P],
                                     wo_sb[:, bass.ds(e, 1), c, :], start=(c == 0), stop=(c == MC - 1))
                last.then_inc(s_y, 1)

            pe.wait_ge(s_big, 16 * 3 * E)
            pe.wait_ge(s_eid, 1)
            rows_turn(0, 0)
            hidden(0, 0, expert(0, 0))
            rows_turn(0, 1)
            inter_turn(0, 0)

            def step_tile(kk, r, last=False):
                hidden(kk, r, expert(kk, r))
                if not last:
                    rows_turn(kk, r + 1)
                down(kk, r - 1, expert(kk, r - 1))
                inter_turn(kk, r)

            step_tile(0, 1)
            with pe.Fori(0, LOOPS) as kk:
                for r in range(2, 2 + ROW_BUFS):
                    step_tile(kk, r)
            step_tile(0, TILES - 1, last=True)
            down(0, TILES - 1, expert(0, TILES - 1))

        @block.vector
        def _(dve):
            steps = [0]

            def link(ins):
                steps[0] += 1
                ins.then_inc(s_dve, 1)
                dve.wait_ge(s_dve, steps[0])

            def bcast(ap, shape):
                return ap.to_broadcast(shape)

            def statistics(norm, b, k):
                link(dve.bn_stats(stats[:, norm, k, :], x_sb[:, b % 2, k, :]))
                ins = dve.bn_aggr(mv[:, norm, b % 2, k, :], stats[:, norm, k, :])
                if k == KT - 1:
                    ins.then_inc(s_var, 1)

            def refine(norm, b, nth):
                dve.wait_ge(s_r0, nth)
                dve.wait_ge(s_var, nth)
                y0, t = rstd0[:, norm, :], tmp[:, norm, :]
                link(dve.tensor_tensor(t, y0, y0, ALU.mult))
                link(dve.scalar_tensor_tensor(out=t, in0=mv[:, norm, b % 2, :, 1], scalar=EPS, in1=t,
                                              op0=ALU.add, op1=ALU.mult))
                link(dve.tensor_scalar(t, t, -0.5, 1.5, ALU.mult, ALU.add))
                link(dve.tensor_tensor(rstd[:, norm, b % 2, :], t, y0, ALU.mult))

            def first_norm(b):
                dve.wait_ge(s_x[b], 16)
                for k in range(KT):
                    statistics(0, b, k)

            def scores_in(b, nth):
                refine(0, b, nth)
                link(dve.tensor_scalar(esc[:, b % 2, :], rstd[:, 0, b % 2, :], scale, None, ALU.mult))
                for k in range(KT):
                    i = KT * b + k
                    dve.wait_ge(s_sc, i + 1)
                    s = prob[:, b % 2, k, :]
                    dve.scalar_tensor_tensor(out=s, in0=x_sb[:, b % 2, k, :], scalar=mv[:, 0, b % 2, k, 0:1],
                                             in1=ps_score[i % 3][:, :], op0=ALU.subtract,
                                             op1=ALU.mult).then_inc(s_t1, 1)
                    dve.wait_ge(s_t1, i + 1)
                    dve.wait_ge(s_mf, i + 1)
                    dve.tensor_tensor_reduce(s, s, mask_f[:, i % 4, :], 1.0, -3e38, ALU.add, ALU.max,
                                             smax[:, b % 2, k:k + 1]).then_inc(s_t2, 1)
                    dve.wait_ge(s_t2, i + 1)
                    dve.scalar_tensor_tensor(out=ebi[:, b % 2, k:k + 1], in0=smax[:, b % 2, k:k + 1], scalar=-1.0,
                                             in1=esc[:, b % 2, k:k + 1], op0=ALU.mult,
                                             op1=ALU.mult).then_inc(s_aff, 1)

            def residual(b):
                dve.wait_ge(s_e, KT * (b + 1))
                link(dve.tensor_scalar(live[:, :], smax[:, b % 2, :], ALL_MASKED, None, ALU.is_gt))
                link(dve.tensor_tensor(coef[:, :], esum[:, b % 2, :], live[:, :], ALU.mult))
                link(dve.reciprocal(coef[:, :], coef[:, :]))
                link(dve.tensor_tensor(coef[:, :], coef[:, :], live[:, :], ALU.mult))
                link(dve.tensor_scalar(coef[:, :], coef[:, :], tgates[:, 0:1], None, ALU.mult))
                for k in range(KT):
                    dve.scalar_tensor_tensor(out=x_sb[:, b % 2, k, :], in0=prob[:, b % 2, k, :],
                                             scalar=coef[:, k:k + 1], in1=x_sb[:, b % 2, k, :], op0=ALU.mult,
                                             op1=ALU.add).then_inc(s_x1, 1)
                    dve.wait_ge(s_x1, KT * b + k + 1)
                    statistics(1, b, k)

            def second_norm(b, nth):
                refine(1, b, nth)
                dve.scalar_tensor_tensor(out=shift[:, b % 2, :], in0=mv[:, 1, b % 2, :, 0], scalar=-1.0,
                                         in1=rstd[:, 1, b % 2, :], op0=ALU.mult, op1=ALU.mult).then_inc(s_sh, 1)

            def top2(b):
                dve.wait_ge(s_lg, KT * (b + 1))
                dve.tensor_copy(logit[:, :, :], ps_logit[:, 0:KT * E].rearrange("p (k e) -> p k e", e=E))\
                   .then_inc(s_lgc, 1)
                dve.wait_ge(s_lgc, b + 1)
                full = [P, KT, E]
                em = bcast(expert_m[:, :].unsqueeze(1), full)
                for c in range(TOP_K):
                    one = chose[:, c, b * KT:(b + 1) * KT, :]
                    link(dve.tensor_reduce(best[:, c, :], logit[:, :, :], AX_X, ALU.max))
                    link(dve.tensor_tensor(eq[:, :, :], logit[:, :, :], bcast(best[:, c, :].unsqueeze(2), full),
                                           ALU.is_equal))
                    link(dve.tensor_tensor(cand[:, :, :], eq[:, :, :], em, ALU.mult))
                    link(dve.tensor_reduce(which[:, :], cand[:, :, :], AX_X, ALU.min))
                    link(dve.tensor_tensor(one, em, bcast(which[:, :].unsqueeze(2), full), ALU.is_equal))
                    if c == 0:
                        link(dve.scalar_tensor_tensor(out=logit[:, :, :], in0=one, scalar=-1e38,
                                                      in1=logit[:, :, :], op0=ALU.mult, op1=ALU.add))
                dve.tensor_tensor(gap[:, :], best[:, 1, :], best[:, 0, :], ALU.subtract).then_inc(s_gap, 1)
                dve.wait_ge(s_egap, b + 1)
                link(dve.tensor_scalar(share[:, 0, :], egap[:, :], 1.0, None, ALU.add))
                link(dve.reciprocal(share[:, 0, :], share[:, 0, :]))
                link(dve.tensor_scalar(share[:, 0, :], share[:, 0, :], tgates[:, 1:2], None, ALU.mult))
                link(dve.tensor_tensor(share[:, 1, :], egap[:, :], share[:, 0, :], ALU.mult))
                one = [chose[:, c, b * KT:(b + 1) * KT, :] for c in range(TOP_K)]
                link(dve.tensor_tensor(eq[:, :, :], one[0], bcast(share[:, 0, :].unsqueeze(2), full), ALU.mult))
                link(dve.tensor_tensor(cand[:, :, :], one[1], bcast(share[:, 1, :].unsqueeze(2), full), ALU.mult))
                if b >= 2:
                    dve.wait_ge(s_wst[b % 2], 16 * (b // 2))
                dve.tensor_tensor(wtok[:, b % 2], eq[:, :, :], cand[:, :, :], ALU.add).then_inc(s_wt, 1)

            dve.wait_ge(s_wT, 1)
            dve.tensor_copy(wqkT[:, :, :].rearrange("p a o -> p (a o)"), ps_xT[0][:, 0:2 * P]).then_inc(s_wTc, 1)
            first_norm(0)
            dve.wait_ge(s_tg, 1)
            for b in range(B):
                scores_in(b, 2 * b + 1 - (b > 0))
                if b + 1 < B:
                    first_norm(b + 1)
                if b == 0:
                    dve.wait_ge(s_const, 4)
                residual(b)
                second_norm(b, 2 * b + 2 + (b + 1 < B))
                if b + 1 < B:
                    pass
                top2(b)

            dve.tensor_tensor(chosen[:, :, :], chose[:, 0].rearrange("p i e -> p e i"),
                              chose[:, 1].rearrange("p i e -> p e i"), ALU.add).then_inc(s_ch, 1)
            dve.wait_ge(s_rank, 1)
            flat = lambda t: t[:, :, :].rearrange("p e i -> p (e i)")
            en = [P, E, NT]
            link(dve.tensor_copy(flat(total), ps_total[:, 0:E * NT]))
            link(dve.tensor_tensor_scan(incl[:, :], flat(total), flat(total), 0.0, ALU.add, ALU.bypass))
            link(dve.tensor_reduce(count[:, :], total[:, :, :], AX_X, ALU.add))
            link(dve.tensor_tensor(cmp_c[:, :, :], bcast(count[:, :].unsqueeze(2), en),
                                   bcast(step_row[:, :].unsqueeze(1), en), ALU.is_gt))
            link(dve.tensor_reduce(ntile[:, :], cmp_c[:, :, :], AX_X, ALU.add))
            link(dve.tensor_tensor_scan(tend[:, :], ntile[:, :], ntile[:, :], 0.0, ALU.add, ALU.bypass))
            link(dve.tensor_tensor(adj[:, :], tend[:, :], ntile[:, :], ALU.subtract))
            link(dve.tensor_scalar(adj[:, :], adj[:, :], float(P), -FAR, ALU.mult, ALU.add))
            last_incl = incl[:, :].rearrange("p (e i) -> p e i", e=E)[:, :, NT - 1]
            link(dve.tensor_tensor(adj[:, :], adj[:, :], last_incl, ALU.subtract))
            link(dve.tensor_tensor(adj[:, :], adj[:, :], count[:, :], ALU.add))
            link(dve.tensor_tensor(flat(place), incl[:, :], flat(total), ALU.subtract))
            link(dve.tensor_tensor(flat(place), flat(place), ps_within[:, 0:E * NT], ALU.add))
            link(dve.tensor_tensor(place[:, :, :], place[:, :, :], bcast(adj[:, :].unsqueeze(2), en), ALU.add))
            for c in range(TOP_K):
                ins = dve.tensor_tensor(pick[:, c], chose[:, c], place[:, :, :].rearrange("p e i -> p i e"), ALU.mult)
            link(ins)
            link(dve.tensor_reduce(pos[:, :], pick[:, :, :, :].rearrange("p c i e -> p (c i) e"), AX_X, ALU.add))
            link(dve.tensor_scalar(pos[:, :], pos[:, :], FAR, None, ALU.add))
            link(dve.tensor_copy(pos_i[:, :], pos[:, :]))
            link(dve.tensor_scalar(hi_i[:, :], pos_i[:, :], 7, None, ALU.arith_shift_right))
            link(dve.tensor_copy(hi[:, :], hi_i[:, :]))
            link(dve.scalar_tensor_tensor(out=lo[:, :], in0=hi[:, :], scalar=-float(P), in1=pos[:, :],
                                          op0=ALU.mult, op1=ALU.add))
            link(dve.tensor_tensor(val[:, :], token_rel[:, :, :].rearrange("p c i -> p (c i)"), lo[:, :],
                                   ALU.subtract))
            for j in range(PAIRS):
                if j >= 4:
                    dve.wait_ge(s_sl, j - 3)
                dve.tensor_scalar(at_lane[:, j % 4, :], lane_row[:, :], lo[:, j:j + 1], None, ALU.is_equal)
                dve.tensor_scalar(at_tile[:, j % 4, :], tile_row[:, :], hi[:, j:j + 1], val[:, j:j + 1],
                                  ALU.is_equal, ALU.mult).then_inc(s_oh, 1)
            te = [P, TILES, E]
            link(dve.tensor_tensor(cmp_t[:, :, :], bcast(tile_row[:, :].unsqueeze(2), te),
                                   bcast(tend[:, :].unsqueeze(1), te), ALU.is_ge))
            link(dve.tensor_reduce(eid[:, :], cmp_t[:, :, :], AX_X, ALU.add))
            link(dve.tensor_scalar(eid[:, :], eid[:, :], float(E - 1), None, ALU.min))
            dve.wait_ge(s_sl, PAIRS)
            dve.tensor_scalar(slot_row[:, :], ps_slot[:, 0:TILES], pad_row[:, 0:1], None, ALU.add).then_inc(s_slot, 1)
            dve.tensor_copy(eid_i[:, :], eid[:, :]).then_inc(s_eid, 1)
            link(dve.tensor_scalar(eid[:, :], eid[:, :], -float(E), None, ALU.add))
            link(dve.tensor_tensor(is_exp[:, :, :], bcast(expert_m[:, :].unsqueeze(1), te),
                                   bcast(eid[:, :].unsqueeze(2), te), ALU.is_equal))

            def slot_weight(kk, r):
                j = ROW_BUFS * kk + r
                q = r % ROW_BUFS
                dve.wait_ge(s_g[q], 16 * (kk + r // ROW_BUFS + 1))
                dve.scalar_tensor_tensor(out=wdump[:, r % 2, :], in0=xg[:, q, D:ROW], scalar=1.0,
                                         in1=is_exp[:, bass.ds(j, 1), :].rearrange("p a e -> p (a e)"),
                                         op0=ALU.mult, op1=ALU.mult,
                                         accum_out=wslot[:, r % 2:r % 2 + 1]).then_inc(s_ws, 1)

            def combine(kk, r):
                j = ROW_BUFS * kk + r
                dve.wait_ge(s_ws, j + 1)
                dve.wait_ge(s_gate, j + 1)
                if r >= 2:
                    dve.wait_ge(s_iT, j - 1)
                dve.scalar_tensor_tensor(out=inter[:, r % 2, :], in0=gate[:, r % 2, :], scalar=wslot[:, r % 2:r % 2 + 1],
                                         in1=ps_h[r % 2][:, M:2 * M], op0=ALU.mult, op1=ALU.mult).then_inc(s_in, 1)

            def inter_out(kk, r):
                j = ROW_BUFS * kk + r
                dve.wait_ge(s_iT, j + 1)
                if r >= 2:
                    dve.wait_ge(s_y, j - 1)
                dve.tensor_copy(interT[:, r % 2, :], ps_iT[r % 2][:, 0:M]).then_inc(s_iTc, 1)

            def y_out(kk, r):
                j = ROW_BUFS * kk + r
                dve.wait_ge(s_y, j + 1)
                if r >= 2:
                    dve.wait_ge(s_sct, 16 * (j - 1))
                dve.tensor_copy(y_sb[:, r % 2, :], ps_y[r % 2][:, :]).then_inc(s_yc, 1)

            slot_weight(0, 0)
            combine(0, 0)
            inter_out(0, 0)

            def step_tile(kk, r):
                slot_weight(kk, r)
                combine(kk, r)
                y_out(kk, r - 1)
                inter_out(kk, r)

            step_tile(0, 1)
            with dve.Fori(0, LOOPS) as kk:
                for r in range(2, 2 + ROW_BUFS):
                    step_tile(kk, r)
            step_tile(0, TILES - 1)
            y_out(0, TILES - 1)


_INS = ['x', 'ctx_512', 'mask_SxS2_bk1', 'mask_BxS2_bf0', 'g_xattn', 'g_ffn', 'L0_xattn_Wq', 'L0_xattn_bq',
        'L0_xattn_Wk', 'L0_xattn_bk', 'L0_ffn_w_gate', 'L0_ffn_wi_0', 'L0_ffn_wi_1', 'L0_ffn_wo']


def kernel(**inputs):
    import numpy as _np
    import concourse.bacc as _bacc
    from concourse import mybir as _mybir
    from concourse.bass_utils import run_bass_kernel_spmd as _run

    nc = _bacc.Bacc("TRN2", target_bir_lowering=False, num_devices=1)
    arrays, args = {}, []
    for name in _INS:
        a = _np.ascontiguousarray(inputs[name])
        arrays[f"in_{name}_dram"] = a
        args.append(nc.dram_tensor(f"in_{name}_dram", a.shape, _mybir.dt.from_np(a.dtype), kind="ExternalInput").ap())
    B, S, D = inputs['x'].shape
    E = inputs['L0_ffn_w_gate'].shape[1]
    out = nc.dram_tensor("out_0_dram", (B * S + P, D), F32, kind="ExternalOutput").ap()
    rows = nc.dram_tensor("normed_rows", (B * S + P, D + E), F32, kind="Internal").ap()
    gated_attention_moe(nc, *args, out, rows)
    r = _run(nc, [arrays], core_ids=[0])
    return r.results[0]["out_0_dram"][:B * S].reshape(B, S, D)
```

```python
from contextlib import ExitStack

import concourse.bass as bass
from concourse import mybir

F32 = mybir.dt.float32
BF16 = mybir.dt.bfloat16
I32 = mybir.dt.int32
U8 = mybir.dt.uint8
ALU = mybir.AluOpType
ACT = mybir.ActivationFunctionType
AX_X = mybir.AxisListType.X

P = 128
MASKED = -1e30
ALL_MASKED = -5e29
FAR_TILE = 512
RSQRT_MAGIC = 0x5F3759DF
EPS = 1e-5
TOP_K = 2
ROW_BUFS = 4


def dims(x, ctx, w_gate, wi_0):
    B, S, D = x.shape
    E, M = w_gate.shape[1], wi_0.shape[2]
    tokens = B * S
    return dict(
        B=B, S=S, D=D, H=ctx.shape[2], E=E, M=M, tokens=tokens, KT=S // P, NT=tokens // P,
        DC=D // P, MC=M // P, ROW=D + E,
        TILES=(TOP_K * tokens + E * (P - 1)) // P,
    )


def gated_attention_moe(nc, x, ctx_in, mask_st, mask_bt, g_attn, g_ffn, wq, bq, wk, bk,
                        w_gate, wi_0, wi_1, wo, out, rows):
    n = dims(x, ctx_in, w_gate, wi_0)
    B, S, D, H, E, M = (n[k] for k in ("B", "S", "D", "H", "E", "M"))
    tokens, KT, NT, DC, MC, ROW, TILES = (n[k] for k in ("tokens", "KT", "NT", "DC", "MC", "ROW", "TILES"))
    scale = float(H) ** -0.5
    PAIRS = TOP_K * NT
    LOOPS = (TILES - 3) // ROW_BUFS
    assert H == P and D == 512 and M == 256 and 1 + LOOPS * ROW_BUFS + 2 == TILES

    with ExitStack() as ctx:
        def sb(name, shape, dt=F32):
            return ctx.enter_context(nc.sbuf_tensor(name, shape, dt))

        def sem(name):
            return ctx.enter_context(nc.semaphore(name))

        bank = [ctx.enter_context(nc.psum_tensor(f"bank{i}", [P, 512], F32)) for i in range(8)]

        ident = sb("ident", [P, P])
        ident_h = sb("ident_h", [P, P], BF16)
        batch_sel = sb("batch_sel", [B, B, P], BF16)
        upper = sb("upper", [P, P], BF16)
        ones = sb("ones", [P, P], BF16)
        lane_row = sb("lane_row", [P, P])
        tile_row = sb("tile_row", [P, TILES])
        tile_far = sb("tile_far", [P, TILES])
        expert_m = sb("expert_m", [P, E])
        step_row = sb("step_row", [P, NT])
        token_rel = sb("token_rel", [P, TOP_K, NT])
        pad_row = sb("pad_row", [P, 1])
        zero_rows = sb("zero_rows", [P, ROW])
        wqk = sb("wqk", [P, 2, P])
        wqkT = sb("wqkT", [P, 2, P])
        bqk = sb("bqk", [P, 2])
        gates = sb("gates", [P, 2])
        tgates = sb("tgates", [P, 2])
        wg_sb = sb("wg_sb", [P, DC, E])
        wi_sb = sb("wi_sb", [P, E, DC, 2 * M])
        wo_sb = sb("wo_sb", [P, E, MC, D])
        m8 = sb("m8", [P, KT, S], U8)
        kp8 = sb("kp8", [B, S], U8)
        mask_s = sb("mask_s", [P, KT, S], BF16)
        mask_b = sb("mask_b", [B, S], BF16)
        x_sb = sb("x_sb", [P, B, KT, S])
        c_sb = sb("c_sb", [P, B, KT, P])
        cT = sb("cT", [P, S])
        qkT = sb("qkT", [P, 2, 2, S])
        prob = sb("prob", [P, 2, KT, S])
        xn = sb("xn", [P, 2, KT, D])
        xnT = sb("xnT", [P, 2, DC, P])
        stats = sb("stats", [P, 8, 6])
        mv = sb("mv", [P, 2, NT, 2])
        veps = sb("veps", [P, 2, NT])
        guess = sb("guess", [P, 2, NT])
        tmp = sb("tmp", [P, 2, NT])
        rstd = sb("rstd", [P, 2, NT])
        shift = sb("shift", [P, NT])
        smax = sb("smax", [P, NT])
        esc = sb("esc", [P, NT])
        ebi = sb("ebi", [P, NT])
        esum = sb("esum", [P, NT])
        live = sb("live", [P, NT])
        coef = sb("coef", [P, NT])
        logit = sb("logit", [P, NT, E])
        cand = sb("cand", [P, NT, E])
        eq = sb("eq", [P, NT, E])
        best = sb("best", [P, 2, NT])
        which = sb("which", [P, NT])
        gap = sb("gap", [P, NT])
        tgap = sb("tgap", [P, NT])
        share = sb("share", [P, 2, NT])
        wparts = sb("wparts", [P, 2, NT, E])
        wtok = sb("wtok", [P, NT, E])
        chose = sb("chose", [P, TOP_K, NT, E])
        chosen = sb("chosen", [P, E, NT], BF16)
        total = sb("total", [P, E, NT])
        incl = sb("incl", [P, E * NT])
        count = sb("count", [P, E])
        cmp_c = sb("cmp_c", [P, E, NT])
        ntile = sb("ntile", [P, E])
        tend = sb("tend", [P, E])
        adj = sb("adj", [P, E])
        place = sb("place", [P, E, NT])
        old_c = c_sb[:, :, :, :].rearrange("p b k h -> p (b k h)")
        pick = old_c[:, 0:PAIRS * E].rearrange("p (c i e) -> p c i e", c=TOP_K, e=E)
        pos = sb("pos", [P, PAIRS])
        pos_i = sb("pos_i", [P, PAIRS], I32)
        hi_i = sb("hi_i", [P, PAIRS], I32)
        hi = sb("hi", [P, PAIRS])
        lo = sb("lo", [P, PAIRS])
        val = sb("val", [P, PAIRS])
        slot_row = sb("slot_row", [P, TILES], I32)
        cmp_t = old_c[:, PAIRS * E:PAIRS * E + TILES * E].rearrange("p (t e) -> p t e", e=E)
        eid = sb("eid", [P, TILES])
        eid_i = sb("eid_i", [P, TILES], I32)
        is_exp = sb("is_exp", [P, TILES, E])
        gidx = sb("gidx", [P, ROW_BUFS], I32)
        sidx = sb("sidx", [P, 2], I32)
        xg = xn[:, :, :, :].rearrange("p a k d -> p (a k d)")[:, 0:ROW_BUFS * ROW]\
            .rearrange("p (q n) -> p q n", q=ROW_BUFS)
        old_prob = prob[:, :, :, :].rearrange("p a k d -> p (a k d)")

        def reuse(start, width):
            return old_prob[:, start:start + 2 * width].rearrange("p (a n) -> p a n", a=2)

        at_lane = old_prob.rearrange("p (c l) -> p c l", l=P)
        at_tile = x_sb[:, 0].rearrange("p k d -> p (k d)")[:, 0:PAIRS * TILES].rearrange("p (c t) -> p c t", t=TILES)
        xgT = reuse(0, D)
        y_sb = reuse(2 * D, D)
        gate = reuse(4 * D, M)
        inter = reuse(4 * D + 2 * M, M)
        interT = reuse(4 * D + 4 * M, M)
        wdump = sb("wdump", [P, 2, E])
        wslot = sb("wslot", [P, 2])

        ps_score, ps_mask = bank[0:2], bank[2:4]
        ps_cT, ps_q, ps_k = bank[4], bank[5], bank[4]
        ps_xT = bank[6]
        ps_logit = bank[7]
        ps_within, ps_total, ps_slot = bank[0], bank[1], bank[4]
        ps_h, ps_gT, ps_iT, ps_y = bank[0:2], bank[2:4], bank[4:6], bank[6:8]

        s_w = sem("small_weights_loaded")
        s_gl = sem("gates_loaded")
        s_m8 = sem("mask_loaded")
        s_kp = sem("padding_mask_loaded")
        s_x = [sem(f"x_loaded_{i}") for i in range(B + 1)]
        s_c = [sem(f"ctx_loaded_{b}") for b in range(B)]
        s_big = sem("expert_weights_loaded")
        s_const = sem("constants_made")
        s_bconst = sem("routing_constants_made")
        s_pool = sem("pool_step")
        s_tg = sem("gates_squashed")
        s_ms = sem("mask_addends_made")
        s_mb = sem("padding_addends_made")
        s_wT = sem("wqk_transposed")
        s_wTc = sem("wqk_copied")
        s_cT = sem("ctx_transposed")
        s_cTc = sem("ctx_copied")
        s_q = sem("q_projected")
        s_k = sem("k_projected")
        s_qc = sem("q_biased")
        s_kc = sem("k_biased")
        s_sc = sem("scores_and_mask_made")
        s_t1 = sem("scores_taken")
        s_t2 = sem("mask_taken")
        s_dve = sem("dve_step")
        s_aff = sem("exp_operands_ready")
        s_e = sem("exp_done")
        s_den = sem("denominators_ready")
        s_rec = sem("denominators_inverted")
        s_x1p = sem("x1_done_by_pool")
        s_x1v = sem("x1_done_by_vector")
        s_gs = sem("rsqrt_guessed")
        s_coef = sem("coefficients_ready")
        s_sh = sem("norm_operands_ready")
        s_xn = sem("xn_done")
        s_xT = sem("xn_transposed")
        s_xTc = sem("xnT_copied")
        s_lg = sem("logits_made")
        s_best = sem("top2_found")
        s_gap = sem("gap_ready")
        s_tgap = sem("gap_squashed")
        s_wt = sem("token_weights_ready")
        s_x1st = [sem(f"x1_stored_{b}") for b in range(B)]
        s_xnst = [sem(f"xn_stored_{i}") for i in range(2)]
        s_wst = sem("token_weights_stored")
        s_zst = sem("padding_stored")
        s_ch = sem("chosen_ready")
        s_rank = sem("ranks_made")
        s_lo = sem("slots_ready")
        s_at = sem("tile_onehots_ready")
        s_oh = sem("lane_onehots_ready")
        s_sl = sem("pair_summed")
        s_slot = sem("slot_rows_ready")
        s_eid = sem("tile_experts_ready")
        s_g = [sem(f"rows_gathered_{i}") for i in range(ROW_BUFS)]
        s_gT = sem("rows_transposed")
        s_gTc = sem("rowsT_copied")
        s_h = sem("hidden_made")
        s_gate = sem("gate_done")
        s_ws = sem("slot_weight_ready")
        s_in = sem("inter_done")
        s_iT = sem("inter_transposed")
        s_iTc = sem("interT_copied")
        s_y = sem("y_made")
        s_yc = sem("y_copied")
        s_sct = sem("y_scattered")
        s_gi = sem("gather_index_ready")
        s_si = sem("scatter_index_ready")
        s_pass = sem("waits_passed")

        block = ctx.enter_context(nc.Block())

        out_v = out[0:tokens, :].rearrange("(b k p) d -> b p k d", b=B, p=P)
        xn_v = rows[0:tokens, 0:D].rearrange("(b k p) d -> b p k d", b=B, p=P)
        wt_v = rows[0:tokens, D:ROW].rearrange("(i p) e -> p i e", p=P)
        POOL_X1 = [list(range(KT))] * (B - 1) + [list(range(KT // 2, KT))]

        def pool_x1_by(b, k):
            mine = sum(len(POOL_X1[c]) for c in range(b)) + sum(q <= k for q in POOL_X1[b])
            return mine, KT * b + k + 1 - mine

        def await_x1(eng, b, k):
            mine, theirs = pool_x1_by(b, k)
            if mine:
                eng.wait_ge(s_x1p, mine)
            if theirs:
                eng.wait_ge(s_x1v, theirs)

        def await_x(eng, b):
            for i in (range(2) if b == 0 else [b + 1]):
                eng.wait_ge(s_x[i], 16)

        def tiles(t, b):
            return t[:, b * KT:(b + 1) * KT]

        @block.sync
        def _(sp):
            half = KT // 2
            x0 = x[0].rearrange("(k p) d -> p k d", p=P)
            for b in range(B):
                sp.dma_start(c_sb[:, b], ctx_in[b].rearrange("(k p) h -> p k h", p=P)).then_inc(s_c[b], 16)
                if b == 0:
                    for i in range(2):
                        sp.dma_start(x_sb[:, 0, i * half:(i + 1) * half], x0[:, i * half:(i + 1) * half, :])\
                          .then_inc(s_x[i], 16)
                    sp.dma_start(m8[:, :, :], mask_st.rearrange("(k p) t -> p k t", p=P)).then_inc(s_m8, 16)
                else:
                    sp.dma_start(x_sb[:, b], x[b].rearrange("(k p) d -> p k d", p=P)).then_inc(s_x[b + 1], 16)
            for e in range(E):
                sp.dma_start(wi_sb[:, e, :, 0:M], wi_0[e].rearrange("(c p) m -> p c m", p=P)).then_inc(s_big, 16)
                sp.dma_start(wi_sb[:, e, :, M:2 * M], wi_1[e].rearrange("(c p) m -> p c m", p=P)).then_inc(s_big, 16)
                sp.dma_start(wo_sb[:, e, :, :], wo[e].rearrange("(c p) d -> p c d", p=P)).then_inc(s_big, 16)

        @block.gpsimd
        def _(pool):
            step = [0]

            def link(ins):
                step[0] += 1
                ins.then_inc(s_pool, 1)
                pool.wait_ge(s_pool, step[0])

            def eye(t, pattern, fill=1.0, compare=ALU.not_equal):
                return pool.affine_select(out=t, in_=t, compare_op=compare, fill=fill, base=0, pattern=pattern,
                                          channel_multiplier=-1)

            pool.memset(batch_sel[:, :, :], 0.0)
            pool.memset(ident_h[:, :], 0.0)
            link(pool.memset(ident[:, :], 0.0))
            eye(ident[:, :], [[1, P]]).then_inc(s_const, 1)
            eye(ident_h[:, :], [[1, P]])
            eye(batch_sel[:, :, :], [[1, B], [0, P]]).then_inc(s_const, 1)
            pool.dma_start(kp8[:, :], mask_bt).then_inc(s_kp, 16)
            pool.dma_start(gates[:, 0:1], g_attn.partition_broadcast(P)).then_inc(s_gl, 16)
            pool.dma_start(gates[:, 1:2], g_ffn.partition_broadcast(P)).then_inc(s_gl, 16)
            pool.iota(expert_m[:, :], [[1, E]], base=-E, channel_multiplier=0, allow_small_or_imprecise_dtypes=True)
            link(pool.memset(upper[:, :], 1.0))
            eye(upper[:, :], [[1, P]], fill=0.0, compare=ALU.is_gt)
            pool.memset(ones[:, :], 1.0)
            for t, pattern, base, mult in (
                (lane_row, [[1, P]], 0, 0), (tile_row, [[1, TILES]], 0, 0), (tile_far, [[1, TILES]], -FAR_TILE, 0),
                (step_row, [[P, NT]], 0, 0), (token_rel, [[0, TOP_K], [P, NT]], -tokens, 1),
                (pad_row, [[0, 1]], tokens, 1),
            ):
                pool.iota(t[:], pattern, base=base, channel_multiplier=mult, allow_small_or_imprecise_dtypes=True)
            link(pool.memset(zero_rows[:, :], 0.0))
            pool.dma_start(rows[tokens:tokens + P, :], zero_rows[:, :]).then_inc(s_zst, 16)
            pool.dma_start(out[tokens:tokens + P, :], zero_rows[:, 0:D]).then_inc(s_zst, 16)
            pool.memset(pos_i[:, :], 0).then_inc(s_bconst, 1)

            def newton(b):
                pool.wait_ge(s_gs, b + 1)
                v, y, t = tiles(veps[:, 1], b), tiles(guess[:, 1], b), tiles(tmp[:, 1], b)
                for n in range(3):
                    link(pool.tensor_tensor(t, y, y, ALU.mult))
                    link(pool.tensor_tensor(t, t, v, ALU.mult))
                    link(pool.tensor_scalar(t, t, -0.5, 1.5, ALU.mult, ALU.add))
                    link(pool.tensor_tensor(tiles(rstd[:, 1], b) if n == 2 else y, t, y, ALU.mult))
                link(pool.tensor_tensor(t, tiles(mv[:, 1, :, 0], b), tiles(rstd[:, 1], b), ALU.mult))
                pool.tensor_scalar(tiles(shift, b), t, -1.0, None, ALU.mult).then_inc(s_sh, 1)

            pool.wait_ge(s_tg, 1)
            for b in range(B + 1):
                if b < B:
                    lv, cf = tiles(live, b), tiles(coef, b)
                    pool.wait_ge(s_t2, KT * (b + 1))
                    link(pool.tensor_scalar(lv, tiles(smax, b), ALL_MASKED, None, ALU.is_gt))
                    pool.wait_ge(s_e, KT * (b + 1))
                    pool.tensor_tensor(cf, tiles(esum, b), lv, ALU.mult).then_inc(s_den, 1)
                    pool.wait_ge(s_rec, b + 1)
                    link(pool.tensor_tensor(cf, cf, lv, ALU.mult))
                    pool.tensor_scalar(cf, cf, tgates[:, 0:1], None, ALU.mult).then_inc(s_coef, 1)
                    pool.wait_ge(s_coef, b + 1)
                if b >= 1:
                    newton(b - 1)
                if b < B:
                    for k in POOL_X1[b]:
                        link(pool.tensor_scalar(prob[:, b % 2, k, :], prob[:, b % 2, k, :],
                                                coef[:, b * KT + k:b * KT + k + 1], None, ALU.mult))
                        pool.tensor_tensor(x_sb[:, b, k, :], prob[:, b % 2, k, :], x_sb[:, b, k, :],
                                           ALU.add).then_inc(s_x1p, 1)

            full = [P, NT, E]
            pool.wait_ge(s_best, 1)
            pool.tensor_tensor(gap[:, :], best[:, 0, :], best[:, 1, :], ALU.subtract).then_inc(s_gap, 1)
            pool.wait_ge(s_tgap, 1)
            for c, sign in enumerate((0.5, -0.5)):
                link(pool.tensor_scalar(share[:, c, :], tgap[:, :], sign, 0.5, ALU.mult, ALU.add))
                link(pool.tensor_scalar(share[:, c, :], share[:, c, :], tgates[:, 1:2], None, ALU.mult))
                link(pool.tensor_tensor(wparts[:, c], chose[:, c], share[:, c, :].unsqueeze(2).to_broadcast(full),
                                        ALU.mult))
            pool.tensor_tensor(wtok[:, :, :], wparts[:, 0], wparts[:, 1], ALU.add).then_inc(s_wt, 1)

            pt = [P, PAIRS, TILES]
            pool.wait_ge(s_lo, 1)
            pool.tensor_tensor(at_tile[:, :, :], at_tile[:, :, :], val[:, :].unsqueeze(2).to_broadcast(pt),
                               ALU.mult).then_inc(s_at, 1)

            pool.wait_ge(s_slot, 1)
            pool.wait_ge(s_zst, 32)
            pool.wait_ge(s_wst, 16)
            for i in range(2):
                pool.wait_ge(s_xnst[i], 16 * (B // 2))
            for b in range(B):
                pool.wait_ge(s_x1st[b], 16)

            def waited():
                pool.sem_inc(s_pass, 1)

            def gather(kk, r):
                q = r % ROW_BUFS
                pool.tensor_copy(gidx[:, q:q + 1], slot_row[:, bass.ds(ROW_BUFS * kk + r, 1)]).then_inc(s_gi, 1)
                pool.wait_ge(s_gi, ROW_BUFS * kk + r + 1)
                waited()
                pool.indirect_dma_start(xg[:, q, :], None, rows,
                                        bass.IndirectOffsetOnAxis(ap=gidx[:, q:q + 1], axis=0)).then_inc(s_g[q], 16)

            def scatter(kk, r):
                q = r % 2
                pool.tensor_copy(sidx[:, q:q + 1], slot_row[:, bass.ds(ROW_BUFS * kk + r, 1)]).then_inc(s_si, 1)
                pool.wait_ge(s_si, ROW_BUFS * kk + r + 1)
                pool.wait_ge(s_yc, ROW_BUFS * kk + r + 1)
                waited()
                pool.indirect_dma_start(out, bass.IndirectOffsetOnAxis(ap=sidx[:, q:q + 1], axis=0), y_sb[:, q, :],
                                        None, compute_op=ALU.add).then_inc(s_sct, 16)
                pool.wait_ge(s_sct, 16 * (ROW_BUFS * kk + r + 1))

            for r in range(ROW_BUFS):
                gather(0, r)
            turns = (TILES - ROW_BUFS) // ROW_BUFS
            with pool.Fori(0, turns) as kk:
                for r in range(ROW_BUFS):
                    scatter(kk, r)
                    gather(kk, r + ROW_BUFS)
            for j in range(turns * ROW_BUFS, TILES):
                scatter(0, j)
                if j + ROW_BUFS < TILES:
                    gather(0, j + ROW_BUFS)

        @block.scalar
        def _(act):
            act.dma_start(wqk[:, 0, :], wq).then_inc(s_w, 16)
            act.dma_start(wqk[:, 1, :], wk).then_inc(s_w, 16)
            act.dma_start(bqk[:, 0:1], bq.rearrange("(o a) -> o a", a=1)).then_inc(s_w, 16)
            act.dma_start(bqk[:, 1:2], bk.rearrange("(o a) -> o a", a=1)).then_inc(s_w, 16)
            act.dma_start(wg_sb[:, :, :], w_gate.rearrange("(c p) e -> p c e", p=P)).then_inc(s_w, 16)

            def project_out(b):
                act.wait_ge(s_cT, b + 1)
                if b >= 1:
                    act.wait_ge(s_k, b)
                act.activation(cT[:, :], ps_cT[:, :], ACT.Copy).then_inc(s_cTc, 1)
                if b >= 2:
                    act.wait_ge(s_sc, KT * (b - 1))
                act.wait_ge(s_q, b + 1)
                act.activation(qkT[:, b % 2, 0, :], ps_q[:, :], ACT.Identity, bias=bqk[:, 0:1]).then_inc(s_qc, 1)
                act.wait_ge(s_k, b + 1)
                act.activation(qkT[:, b % 2, 1, :], ps_k[:, :], ACT.Identity, bias=bqk[:, 1:2]).then_inc(s_kc, 1)

            def exp(b, k):
                i = KT * b + k
                act.wait_ge(s_aff, i + 1)
                act.activation(prob[:, b % 2, k, :], prob[:, b % 2, k, :], ACT.Exp, scale=esc[:, i:i + 1],
                               bias=ebi[:, i:i + 1], accum_out=esum[:, i:i + 1]).then_inc(s_e, 1)

            def store_x1(b):
                await_x1(act, b, KT - 1)
                act.dma_start(out_v[b], x_sb[:, b]).then_inc(s_x1st[b], 16)

            def norm(b, k):
                i = KT * b + k
                if k == 0:
                    act.wait_ge(s_sh, b + 1)
                    if b >= 2:
                        act.wait_ge(s_xnst[b % 2], 16 * (b // 2))
                        act.wait_ge(s_xT, KT * (b - 1))
                act.activation(xn[:, b % 2, k, :], x_sb[:, b, k, :], ACT.Identity,
                               scale=rstd[:, 1, i:i + 1], bias=shift[:, i:i + 1]).then_inc(s_xn, 1)

            def turned(b, k):
                i = KT * b + k
                act.wait_ge(s_xT, i + 1)
                if i >= 2:
                    act.wait_ge(s_lg, i - 1)
                act.activation(xnT[:, i % 2].rearrange("p c t -> p (c t)"), ps_xT[:, :], ACT.Copy).then_inc(s_xTc, 1)

            def store_xn(b):
                act.wait_ge(s_xn, KT * (b + 1))
                act.dma_start(xn_v[b], xn[:, b % 2]).then_inc(s_xnst[b % 2], 16)

            act.wait_ge(s_wT, 1)
            act.activation(wqkT[:, :, :].rearrange("p a o -> p (a o)"), ps_xT[:, 0:2 * P], ACT.Copy).then_inc(s_wTc, 1)
            act.wait_ge(s_w, 16 * 5)
            project_out(0)
            act.wait_ge(s_kp, 16)
            act.activation(mask_b[:, :], kp8[:, :], ACT.Copy, scale=MASKED).then_inc(s_mb, 1)
            act.wait_ge(s_m8, 16)
            for k in range(KT):
                act.activation(mask_s[:, k, :], m8[:, k, :], ACT.Copy, scale=MASKED).then_inc(s_ms, 1)
            act.wait_ge(s_gl, 32)
            act.activation(tgates[:, :], gates[:, :], ACT.Tanh).then_inc(s_tg, 1)
            for b in range(B + 2):
                if b + 1 < B:
                    project_out(b + 1)
                for k in range(KT):
                    if b < B:
                        exp(b, k)
                    if b >= 2:
                        norm(b - 2, k)
                        turned(b - 2, k)
                if b >= 2:
                    store_xn(b - 2)
                if 1 <= b <= B:
                    store_x1(b - 1)
            act.wait_ge(s_gap, 1)
            act.activation(tgap[:, :], gap[:, :], ACT.Tanh, scale=0.5).then_inc(s_tgap, 1)
            act.wait_ge(s_wt, 1)
            act.dma_start(wt_v, wtok[:, :, :]).then_inc(s_wst, 16)

            def rows_out(kk, r):
                j = ROW_BUFS * kk + r
                act.wait_ge(s_gT, j + 1)
                if r >= 2:
                    act.wait_ge(s_h, j - 1)
                act.activation(xgT[:, r % 2, :], ps_gT[r % 2][:, :], ACT.Copy).then_inc(s_gTc, 1)

            def silu(kk, r):
                j = ROW_BUFS * kk + r
                act.wait_ge(s_h, j + 1)
                if r >= 2:
                    act.wait_ge(s_in, j - 1)
                act.activation(gate[:, r % 2, :], ps_h[r % 2][:, 0:M], ACT.Silu).then_inc(s_gate, 1)

            rows_out(0, 0)
            rows_out(0, 1)
            silu(0, 0)
            silu(0, 1)
            with act.Fori(0, LOOPS) as kk:
                for r in range(2, 2 + ROW_BUFS):
                    rows_out(kk, r)
                    silu(kk, r)
            rows_out(0, TILES - 1)
            silu(0, TILES - 1)

        @block.tensor
        def _(pe):
            pe.wait_ge(s_w, 16 * 5)
            pe.wait_ge(s_const, 1)
            for i in range(2):
                last = pe.transpose(ps_xT[:, i * P:(i + 1) * P], wqk[:, i, :], ident[:, :])
            last.then_inc(s_wT, 1)

            def project(b):
                pe.wait_ge(s_c[b], 16)
                if b >= 1:
                    pe.wait_ge(s_kc, b)
                for k in range(KT):
                    last = pe.transpose(ps_cT[:, k * P:(k + 1) * P], c_sb[:, b, k, :], ident[:, :])
                last.then_inc(s_cT, 1)
                pe.wait_ge(s_cTc, b + 1)
                if b == 0:
                    pe.wait_ge(s_wTc, 1)
                if b >= 1:
                    pe.wait_ge(s_qc, b)
                pe.matmul(ps_q[:, :], wqkT[:, 0, :], cT[:, :], start=True, stop=True).then_inc(s_q, 1)
                pe.matmul(ps_k[:, :], wqkT[:, 1, :], cT[:, :], start=True, stop=True).then_inc(s_k, 1)

            def score(i):
                b, k = i // KT, i % KT
                if k == 0:
                    pe.wait_ge(s_qc, b + 1)
                    pe.wait_ge(s_kc, b + 1)
                if i >= 2:
                    pe.wait_ge(s_t1, i - 1)
                pe.matmul(ps_score[i % 2][:, :], qkT[:, b % 2, 0, k * P:(k + 1) * P], qkT[:, b % 2, 1, :],
                          start=True, stop=True)
                if i == 0:
                    pe.wait_ge(s_const, 2)
                    pe.wait_ge(s_mb, 1)
                if i < KT:
                    pe.wait_ge(s_ms, i + 1)
                if i >= 2:
                    pe.wait_ge(s_t2, i - 1)
                pe.matmul(ps_mask[i % 2][:, :], ident_h[:, :], mask_s[:, k, :], start=True, stop=False)
                pe.matmul(ps_mask[i % 2][:, :], batch_sel[:, b, :], mask_b[:, :], start=False, stop=True)\
                  .then_inc(s_sc, 1)

            def turn(i):
                b, k = i // KT, i % KT
                pe.wait_ge(s_xn, i + 1)
                if i >= 1:
                    pe.wait_ge(s_xTc, i)
                else:
                    pe.wait_ge(s_wTc, 1)
                for c in range(DC):
                    last = pe.transpose(ps_xT[:, c * P:(c + 1) * P], xn[:, b % 2, k, c * P:(c + 1) * P], ident[:, :])
                last.then_inc(s_xT, 1)

            def route(i):
                pe.wait_ge(s_xTc, i + 1)
                for c in range(DC):
                    last = pe.matmul(ps_logit[:, i * E:(i + 1) * E], xnT[:, i % 2, c, :], wg_sb[:, c, :],
                                     start=(c == 0), stop=(c == DC - 1))
                last.then_inc(s_lg, 1)

            project(0)
            score(0)
            score(1)
            for b in range(B + 2):
                if b + 1 < B:
                    project(b + 1)
                for k in range(KT):
                    i = KT * b + k
                    if i + 2 < NT:
                        score(i + 2)
                    if b >= 2:
                        turn(i - 2 * KT)
                        if k >= 1:
                            route(i - 2 * KT - 1)
                if b >= 2:
                    route(KT * (b - 1) - 1)

            pe.wait_ge(s_bconst, 1)
            pe.wait_ge(s_ch, 1)
            ch = chosen[:, :, :].rearrange("p e i -> p (e i)")
            pe.matmul(ps_total[:, 0:E * NT], ones[:, :], ch, start=True, stop=True)
            pe.matmul(ps_within[:, 0:E * NT], upper[:, :], ch, start=True, stop=True).then_inc(s_rank, 1)
            pe.wait_ge(s_at, 1)
            for j in range(PAIRS):
                if j % 8 == 0:
                    pe.wait_ge(s_oh, j // 8 + 1)
                last = pe.matmul(ps_slot[:, 0:TILES], at_lane[:, j, :], at_tile[:, j, :],
                                 start=(j == 0), stop=(j == PAIRS - 1))
            last.then_inc(s_sl, 1)

            def rows_turn(kk, r):
                j = ROW_BUFS * kk + r
                pe.wait_ge(s_g[r % ROW_BUFS], 16 * (kk + r // ROW_BUFS + 1))
                if r >= 2:
                    pe.wait_ge(s_gTc, j - 1)
                for c in range(DC):
                    last = pe.transpose(ps_gT[r % 2][:, c * P:(c + 1) * P],
                                        xg[:, r % ROW_BUFS, c * P:(c + 1) * P], ident[:, :])
                last.then_inc(s_gT, 1)

            def expert(kk, r):
                return pe.value_load(eid_i[0:1, bass.ds(ROW_BUFS * kk + r, 1)], min_val=0, max_val=E - 1)

            def hidden(kk, r, e):
                j = ROW_BUFS * kk + r
                pe.wait_ge(s_gTc, j + 1)
                if r >= 2:
                    pe.wait_ge(s_in, j - 1)
                for c in range(DC):
                    last = pe.matmul(ps_h[r % 2][:, :], xgT[:, r % 2, c * P:(c + 1) * P],
                                     wi_sb[:, bass.ds(e, 1), c, :], start=(c == 0), stop=(c == DC - 1))
                last.then_inc(s_h, 1)

            def inter_turn(kk, r):
                j = ROW_BUFS * kk + r
                pe.wait_ge(s_in, j + 1)
                if r >= 2:
                    pe.wait_ge(s_iTc, j - 1)
                for c in range(MC):
                    last = pe.transpose(ps_iT[r % 2][:, c * P:(c + 1) * P], inter[:, r % 2, c * P:(c + 1) * P],
                                        ident[:, :])
                last.then_inc(s_iT, 1)

            def down(kk, r, e):
                j = ROW_BUFS * kk + r
                pe.wait_ge(s_iTc, j + 1)
                if r >= 2:
                    pe.wait_ge(s_yc, j - 1)
                for c in range(MC):
                    last = pe.matmul(ps_y[r % 2][:, :], interT[:, r % 2, c * P:(c + 1) * P],
                                     wo_sb[:, bass.ds(e, 1), c, :], start=(c == 0), stop=(c == MC - 1))
                last.then_inc(s_y, 1)

            pe.wait_ge(s_big, 16 * 3 * E)
            pe.wait_ge(s_eid, 1)
            rows_turn(0, 0)
            hidden(0, 0, expert(0, 0))
            rows_turn(0, 1)
            inter_turn(0, 0)

            def step_tile(kk, r, last=False):
                hidden(kk, r, expert(kk, r))
                if not last:
                    rows_turn(kk, r + 1)
                down(kk, r - 1, expert(kk, r - 1))
                inter_turn(kk, r)

            step_tile(0, 1)
            with pe.Fori(0, LOOPS) as kk:
                for r in range(2, 2 + ROW_BUFS):
                    step_tile(kk, r)
            step_tile(0, TILES - 1, last=True)
            down(0, TILES - 1, expert(0, TILES - 1))

        @block.vector
        def _(dve):
            steps = [0]

            def link(ins):
                steps[0] += 1
                ins.then_inc(s_dve, 1)
                dve.wait_ge(s_dve, steps[0])

            def bcast(ap, shape):
                return ap.to_broadcast(shape)

            def statistics(norm, i):
                link(dve.bn_stats(stats[:, i % 8, :], x_sb[:, i // KT, i % KT, :]))
                return dve.bn_aggr(mv[:, norm, i, :], stats[:, i % 8, :])

            def guessed(norm, a, z):
                v, y = veps[:, norm, a:z], guess[:, norm, a:z]
                link(dve.tensor_scalar(v, mv[:, norm, a:z, 1], EPS, None, ALU.add))
                link(dve.tensor_scalar(y.bitcast(I32), v.bitcast(I32), 1, None, ALU.arith_shift_right))
                return dve.tensor_scalar(y.bitcast(I32), y.bitcast(I32), -1.0, float(RSQRT_MAGIC), ALU.mult, ALU.add)

            def first_rstd(a, z):
                link(guessed(0, a, z))
                v, y, t = veps[:, 0, a:z], guess[:, 0, a:z], tmp[:, 0, a:z]
                for n in range(3):
                    link(dve.tensor_tensor(t, y, y, ALU.mult))
                    link(dve.tensor_tensor(t, t, v, ALU.mult))
                    link(dve.tensor_scalar(t, t, -0.5, 1.5, ALU.mult, ALU.add))
                    link(dve.tensor_tensor(rstd[:, 0, a:z] if n == 2 else y, t, y, ALU.mult))
                link(dve.tensor_scalar(esc[:, a:z], rstd[:, 0, a:z], scale, None, ALU.mult))

            def first_norm(b):
                for k in range(KT):
                    if b > 0 and k == 0:
                        dve.wait_ge(s_x[b + 1], 16)
                    elif b == 0 and k % (KT // 2) == 0:
                        dve.wait_ge(s_x[k // (KT // 2)], 16)
                    last = statistics(0, KT * b + k)
                link(last)

            def attend(b):
                for k in range(KT):
                    i = KT * b + k
                    dve.wait_ge(s_sc, i + 1)
                    s = prob[:, b % 2, k, :]
                    if b >= 2 and k == 0:
                        await_x1(dve, b - 2, KT - 1)
                    dve.scalar_tensor_tensor(out=s, in0=x_sb[:, b, k, :], scalar=mv[:, 0, i, 0:1],
                                             in1=ps_score[i % 2][:, :], op0=ALU.subtract,
                                             op1=ALU.mult).then_inc(s_t1, 1)
                    dve.wait_ge(s_t1, i + 1)
                    dve.tensor_tensor_reduce(s, s, ps_mask[i % 2][:, :], 1.0, -3e38, ALU.add, ALU.max,
                                             smax[:, i:i + 1]).then_inc(s_t2, 1)
                    dve.wait_ge(s_t2, i + 1)
                    dve.scalar_tensor_tensor(out=ebi[:, i:i + 1], in0=smax[:, i:i + 1], scalar=-1.0,
                                             in1=esc[:, i:i + 1], op0=ALU.mult, op1=ALU.mult).then_inc(s_aff, 1)

            def invert(b):
                dve.wait_ge(s_den, b + 1)
                dve.reciprocal(tiles(coef, b), tiles(coef, b)).then_inc(s_rec, 1)

            def second_stats(b, ks):
                for k in ks:
                    i = KT * b + k
                    await_x1(dve, b, k)
                    last = statistics(1, i)
                return last

            first_norm(0)
            first_rstd(0, KT)
            for b in range(B):
                attend(b)
                if b == 0:
                    for c in range(1, B):
                        first_norm(c)
                        if c == 1:
                            invert(0)
                    first_rstd(KT, NT)
                else:
                    second_stats(b - 1, range(KT // 2))
                    invert(b)
                    link(second_stats(b - 1, range(KT // 2, KT)))
                    guessed(1, KT * (b - 1), KT * b).then_inc(s_gs, 1)
            dve.wait_ge(s_coef, B)
            own = [k for k in range(KT) if k not in POOL_X1[B - 1]]
            for k in own:
                i = KT * (B - 1) + k
                dve.scalar_tensor_tensor(out=x_sb[:, B - 1, k, :], in0=prob[:, (B - 1) % 2, k, :],
                                         scalar=coef[:, i:i + 1], in1=x_sb[:, B - 1, k, :], op0=ALU.mult,
                                         op1=ALU.add).then_inc(s_x1v, 1)
                link(second_stats(B - 1, [k]))
            link(second_stats(B - 1, POOL_X1[B - 1]))
            guessed(1, KT * (B - 1), NT).then_inc(s_gs, 1)

            dve.wait_ge(s_bconst, 1)
            dve.wait_ge(s_lg, NT)
            link(dve.tensor_copy(logit[:, :, :].rearrange("p i e -> p (i e)"), ps_logit[:, 0:NT * E]))
            full = [P, NT, E]
            em = bcast(expert_m[:, :].unsqueeze(1), full)
            for c in range(TOP_K):
                one = chose[:, c]
                link(dve.tensor_reduce(best[:, c, :], logit[:, :, :], AX_X, ALU.max))
                link(dve.tensor_tensor(eq[:, :, :], logit[:, :, :], bcast(best[:, c, :].unsqueeze(2), full),
                                       ALU.is_equal))
                link(dve.tensor_tensor(cand[:, :, :], eq[:, :, :], em, ALU.mult))
                link(dve.tensor_reduce(which[:, :], cand[:, :, :], AX_X, ALU.min))
                ins = dve.tensor_tensor(one, em, bcast(which[:, :].unsqueeze(2), full), ALU.is_equal)
                if c == 0:
                    link(ins)
                    link(dve.scalar_tensor_tensor(out=logit[:, :, :], in0=one, scalar=-1e38, in1=logit[:, :, :],
                                                  op0=ALU.mult, op1=ALU.add))
                else:
                    ins.then_inc(s_best, 1)
                    dve.wait_ge(s_best, 1)

            dve.tensor_tensor(chosen[:, :, :], chose[:, 0].rearrange("p i e -> p e i"),
                              chose[:, 1].rearrange("p i e -> p e i"), ALU.add).then_inc(s_ch, 1)
            dve.wait_ge(s_rank, 1)
            flat = lambda t: t[:, :, :].rearrange("p e i -> p (e i)")
            en = [P, E, NT]
            link(dve.tensor_copy(flat(total), ps_total[:, 0:E * NT]))
            link(dve.tensor_tensor_scan(incl[:, :], flat(total), flat(total), 0.0, ALU.add, ALU.bypass))
            link(dve.tensor_reduce(count[:, :], total[:, :, :], AX_X, ALU.add))
            link(dve.tensor_tensor(cmp_c[:, :, :], bcast(count[:, :].unsqueeze(2), en),
                                   bcast(step_row[:, :].unsqueeze(1), en), ALU.is_gt))
            link(dve.tensor_reduce(ntile[:, :], cmp_c[:, :, :], AX_X, ALU.add))
            link(dve.tensor_tensor_scan(tend[:, :], ntile[:, :], ntile[:, :], 0.0, ALU.add, ALU.bypass))
            link(dve.tensor_tensor(adj[:, :], tend[:, :], ntile[:, :], ALU.subtract))
            link(dve.tensor_scalar(adj[:, :], adj[:, :], float(P), -float(P * FAR_TILE), ALU.mult, ALU.add))
            last_incl = incl[:, :].rearrange("p (e i) -> p e i", e=E)[:, :, NT - 1]
            link(dve.tensor_tensor(adj[:, :], adj[:, :], last_incl, ALU.subtract))
            link(dve.tensor_tensor(adj[:, :], adj[:, :], count[:, :], ALU.add))
            link(dve.tensor_tensor(flat(place), incl[:, :], flat(total), ALU.subtract))
            link(dve.tensor_tensor(flat(place), flat(place), ps_within[:, 0:E * NT], ALU.add))
            link(dve.tensor_tensor(place[:, :, :], place[:, :, :], bcast(adj[:, :].unsqueeze(2), en), ALU.add))
            for c in range(TOP_K):
                ins = dve.tensor_tensor(pick[:, c], chose[:, c], place[:, :, :].rearrange("p e i -> p i e"), ALU.mult)
            link(ins)
            link(dve.tensor_reduce(pos[:, :], pick[:, :, :, :].rearrange("p c i e -> p (c i) e"), AX_X, ALU.add))
            link(dve.tensor_copy(pos_i[:, :], pos[:, :]))
            link(dve.tensor_scalar(hi_i[:, :], pos_i[:, :], 7, None, ALU.arith_shift_right))
            link(dve.tensor_copy(hi[:, :], hi_i[:, :]))
            link(dve.scalar_tensor_tensor(out=lo[:, :], in0=hi[:, :], scalar=-float(P), in1=pos[:, :],
                                          op0=ALU.mult, op1=ALU.add))
            dve.tensor_tensor(val[:, :], token_rel[:, :, :].rearrange("p c i -> p (c i)"), lo[:, :], ALU.subtract)
            pt, pl = [P, PAIRS, TILES], [P, 8, P]
            dve.wait_ge(s_x1st[0], 16)
            dve.wait_ge(s_xn, KT)
            dve.tensor_tensor(at_tile[:, :, :], bcast(tile_far[:, :].unsqueeze(1), pt),
                              bcast(hi[:, :].unsqueeze(2), pt), ALU.is_equal).then_inc(s_lo, 1)
            for a in range(0, PAIRS, 8):
                dve.tensor_tensor(at_lane[:, a:a + 8, :], bcast(lane_row[:, :].unsqueeze(1), pl),
                                  bcast(lo[:, a:a + 8].unsqueeze(2), pl), ALU.is_equal).then_inc(s_oh, 1)
            te = [P, TILES, E]
            link(dve.tensor_tensor(cmp_t[:, :, :], bcast(tile_row[:, :].unsqueeze(2), te),
                                   bcast(tend[:, :].unsqueeze(1), te), ALU.is_ge))
            link(dve.tensor_reduce(eid[:, :], cmp_t[:, :, :], AX_X, ALU.add))
            link(dve.tensor_scalar(eid[:, :], eid[:, :], float(E - 1), None, ALU.min))
            dve.wait_ge(s_sl, 1)
            dve.tensor_scalar(slot_row[:, :], ps_slot[:, 0:TILES], pad_row[:, 0:1], None, ALU.add).then_inc(s_slot, 1)
            dve.tensor_copy(eid_i[:, :], eid[:, :]).then_inc(s_eid, 1)
            link(dve.tensor_scalar(eid[:, :], eid[:, :], -float(E), None, ALU.add))
            link(dve.tensor_tensor(is_exp[:, :, :], bcast(expert_m[:, :].unsqueeze(1), te),
                                   bcast(eid[:, :].unsqueeze(2), te), ALU.is_equal))

            def slot_weight(kk, r):
                j = ROW_BUFS * kk + r
                q = r % ROW_BUFS
                dve.wait_ge(s_g[q], 16 * (kk + r // ROW_BUFS + 1))
                dve.scalar_tensor_tensor(out=wdump[:, r % 2, :], in0=xg[:, q, D:ROW], scalar=1.0,
                                         in1=is_exp[:, bass.ds(j, 1), :].rearrange("p a e -> p (a e)"),
                                         op0=ALU.mult, op1=ALU.mult,
                                         accum_out=wslot[:, r % 2:r % 2 + 1]).then_inc(s_ws, 1)

            def combine(kk, r):
                j = ROW_BUFS * kk + r
                dve.wait_ge(s_ws, j + 1)
                dve.wait_ge(s_gate, j + 1)
                if r >= 2:
                    dve.wait_ge(s_iT, j - 1)
                dve.scalar_tensor_tensor(out=inter[:, r % 2, :], in0=gate[:, r % 2, :], scalar=wslot[:, r % 2:r % 2 + 1],
                                         in1=ps_h[r % 2][:, M:2 * M], op0=ALU.mult, op1=ALU.mult).then_inc(s_in, 1)

            def inter_out(kk, r):
                j = ROW_BUFS * kk + r
                dve.wait_ge(s_iT, j + 1)
                if r >= 2:
                    dve.wait_ge(s_y, j - 1)
                dve.tensor_copy(interT[:, r % 2, :], ps_iT[r % 2][:, 0:M]).then_inc(s_iTc, 1)

            def y_out(kk, r):
                j = ROW_BUFS * kk + r
                dve.wait_ge(s_y, j + 1)
                if r >= 2:
                    dve.wait_ge(s_sct, 16 * (j - 1))
                dve.tensor_copy(y_sb[:, r % 2, :], ps_y[r % 2][:, :]).then_inc(s_yc, 1)

            slot_weight(0, 0)
            combine(0, 0)
            inter_out(0, 0)

            def step_tile(kk, r):
                slot_weight(kk, r)
                combine(kk, r)
                y_out(kk, r - 1)
                inter_out(kk, r)

            step_tile(0, 1)
            with dve.Fori(0, LOOPS) as kk:
                for r in range(2, 2 + ROW_BUFS):
                    step_tile(kk, r)
            step_tile(0, TILES - 1)
            y_out(0, TILES - 1)


_INS = ['x', 'ctx_512', 'mask_SxS2_bk1', 'mask_BxS2_bf0', 'g_xattn', 'g_ffn', 'L0_xattn_Wq', 'L0_xattn_bq',
        'L0_xattn_Wk', 'L0_xattn_bk', 'L0_ffn_w_gate', 'L0_ffn_wi_0', 'L0_ffn_wi_1', 'L0_ffn_wo']


def kernel(**inputs):
    import numpy as _np
    import concourse.bacc as _bacc
    from concourse import mybir as _mybir
    from concourse.bass_utils import run_bass_kernel_spmd as _run

    nc = _bacc.Bacc("TRN2", target_bir_lowering=False, num_devices=1)
    arrays, args = {}, []
    for name in _INS:
        a = _np.ascontiguousarray(inputs[name])
        arrays[f"in_{name}_dram"] = a
        args.append(nc.dram_tensor(f"in_{name}_dram", a.shape, _mybir.dt.from_np(a.dtype), kind="ExternalInput").ap())
    B, S, D = inputs['x'].shape
    E = inputs['L0_ffn_w_gate'].shape[1]
    out = nc.dram_tensor("out_0_dram", (B * S + P, D), F32, kind="ExternalOutput").ap()
    rows = nc.dram_tensor("normed_rows", (B * S + P, D + E), F32, kind="Internal").ap()
    gated_attention_moe(nc, *args, out, rows)
    r = _run(nc, [arrays], core_ids=[0])
    return r.results[0]["out_0_dram"][:B * S].reshape(B, S, D)
```

```python
from contextlib import ExitStack

import concourse.bass as bass
from concourse import mybir

F32 = mybir.dt.float32
F32R = mybir.dt.float32r
BF16 = mybir.dt.bfloat16
I32 = mybir.dt.int32
U8 = mybir.dt.uint8
ALU = mybir.AluOpType
ACT = mybir.ActivationFunctionType
AX_X = mybir.AxisListType.X

P = 128
MASKED = -1e30
ALL_MASKED = -5e29
RSQRT_MAGIC = 0x5F3759DF
EPS = 1e-5
TOP_K = 2
ROW_BUFS = 4
SOFT_BUFS = 3


def dims(x, ctx, w_gate, wi_0):
    B, S, D = x.shape
    E, M = w_gate.shape[1], wi_0.shape[2]
    tokens = B * S
    return dict(
        B=B, S=S, D=D, H=ctx.shape[2], E=E, M=M, tokens=tokens, KT=S // P, NT=tokens // P,
        DC=D // P, MC=M // P, ROW=D + E,
        TILES=(TOP_K * tokens + E * (P - 1)) // P,
    )


def gated_attention_moe(nc, x, ctx_in, mask_st, mask_bt, g_attn, g_ffn, wq, bq, wk, bk,
                        w_gate, wi_0, wi_1, wo, out, rows):
    n = dims(x, ctx_in, w_gate, wi_0)
    B, S, D, H, E, M = (n[k] for k in ("B", "S", "D", "H", "E", "M"))
    tokens, KT, NT, DC, MC, ROW, TILES = (n[k] for k in ("tokens", "KT", "NT", "DC", "MC", "ROW", "TILES"))
    scale = float(H) ** -0.5
    PAIRS = TOP_K * NT
    LOOPS = (TILES - 3) // ROW_BUFS
    PE_TURNS = 3
    assert H == P and D == 512 and M == 256 and 1 + LOOPS * ROW_BUFS + 2 == TILES and LOOPS % PE_TURNS == 0

    with ExitStack() as ctx:
        def sb(name, shape, dt=F32):
            return ctx.enter_context(nc.sbuf_tensor(name, shape, dt))

        def gone(name, shape, dt=F32):
            with nc.sbuf_tensor(name, shape, dt) as t:
                return t

        def sem(name):
            return ctx.enter_context(nc.semaphore(name))

        bank = [ctx.enter_context(nc.psum_tensor(f"bank{i}", [P, 512], F32)) for i in range(8)]

        ident = sb("ident", [P, P])
        ident_h = sb("ident_h", [P, P], BF16)
        batch_sel = sb("batch_sel", [B, B, P], BF16)
        below = sb("below", [P, P], BF16)
        ones = sb("ones", [P, P], BF16)
        lane_row = sb("lane_row", [P, P], BF16)
        tile_row = sb("tile_row", [P, TILES])
        tile_from1 = sb("tile_from1", [P, TILES], BF16)
        pair_first = sb("pair_first", [P, TOP_K, NT])
        lane = sb("lane", [P, 1])
        expert_m = sb("expert_m", [P, E])
        step_row = sb("step_row", [P, NT])
        wqk = sb("wqk", [P, 2, P])
        wqkT = sb("wqkT", [P, 2, P])
        bqk = sb("bqk", [P, 2])
        gates = sb("gates", [P, 2])
        tgates = sb("tgates", [P, 2])
        wg_sb = sb("wg_sb", [P, DC, E])
        wgc = sb("wgc", [P, DC, E])
        mean_of = sb("mean_of", [P, P])
        wi_sb = gone("wi_sb", [P, E, DC, 2 * M])
        wi_lo = sb("wi_lo", [P, E, DC, 2 * M], F32R)
        before_hi = gone("before_hi", [P, E, DC * 2 * M])
        wi_hi = sb("wi_hi", [P, E, DC, 2 * M], F32R)
        wo_sb = sb("wo_sb", [P, E, MC, D])
        kp8 = sb("kp8", [B, S], U8)
        mask_b = sb("mask_b", [B, S], BF16)

        def early(e):
            return before_hi[:, e]

        X_AT, PROB_AT = (1, 2, 4, 6), (7, 3, 5)
        assert KT * S == DC * 2 * M and len(X_AT) == B and len(PROB_AT) == SOFT_BUFS
        c_sb = early(0).rearrange("p (b k h) -> p b k h", b=B, k=KT)
        x_sb = [early(e).rearrange("p (k d) -> p k d", k=KT) for e in X_AT]
        prob = [early(e).rearrange("p (k d) -> p k d", k=KT) for e in PROB_AT]

        region = gone("region", [P, ROW_BUFS * ROW + 6 * D + 6 * M])
        xg = sb("xg", [P, ROW_BUFS, ROW])
        xgT_hi, xgT_lo = sb("xgT_hi", [P, 2, D], F32R), sb("xgT_lo", [P, 2, D], F32R)
        y_sb, gate = sb("y_sb", [P, 2, D]), sb("gate", [P, 2, M])
        inter, interT = sb("inter", [P, 2, M]), sb("interT", [P, 2, M])
        at = [0]

        def part(words):
            at[0] += words
            return region[:, at[0] - words:at[0]]

        r_xg, r_hi, r_lo, r_y = part(ROW_BUFS * ROW), part(2 * D), part(2 * D), part(2 * D)
        r_gate, r_inter, r_interT = part(2 * M), part(2 * M), part(2 * M)
        x1T = r_xg[:, 0:2 * DC * P].rearrange("p (a c t) -> p a c t", a=2, c=DC)
        cT = r_xg[:, 2 * DC * P:2 * DC * P + S]
        m8 = r_xg[:, 2 * DC * P + S:2 * DC * P + S + KT * S // 4].bitcast(U8).rearrange("p (k t) -> p k t", k=KT)
        qkT = region[:, ROW_BUFS * ROW:ROW_BUFS * ROW + 4 * S].rearrange("p (a q t) -> p a q t", a=2, q=2)
        mask_s = r_y[:, 0:KT * S // 2].bitcast(BF16).rearrange("p (k t) -> p k t", k=KT)
        zero_rows = region[:, ROW_BUFS * ROW + 6 * D + 2 * M:ROW_BUFS * ROW + 6 * D + 2 * M + ROW]
        stats = sb("stats", [P, 8, 6])
        mv = sb("mv", [P, 2, NT, 2])
        veps = sb("veps", [P, 2, NT])
        guess = sb("guess", [P, 2, NT])
        tmp = sb("tmp", [P, 2, NT])
        rstd = sb("rstd", [P, 2, NT])
        shift = sb("shift", [P, NT])
        smax = sb("smax", [P, NT])
        esc = sb("esc", [P, NT])
        ebi = sb("ebi", [P, NT])
        esum = sb("esum", [P, NT])
        live = sb("live", [P, NT])
        coef = sb("coef", [P, NT])
        logit = sb("logit", [P, NT, E])
        cand = sb("cand", [P, NT, E])
        best = sb("best", [P, 2, NT])
        which = sb("which", [P, NT])
        gap = sb("gap", [P, NT])
        tgap = sb("tgap", [P, NT])
        table_trial = sb("table_trial", [P, 1])
        share = sb("share", [P, 2, NT])
        wparts = sb("wparts", [P, 2, NT, E])
        wtok = sb("wtok", [P, NT, E])
        chose = sb("chose", [P, TOP_K, NT, E])
        chosen = sb("chosen", [P, E, NT], BF16)
        total = sb("total", [P, E, NT])
        incl = sb("incl", [P, E * NT])
        count = sb("count", [P, E])
        cmp_c = sb("cmp_c", [P, E, NT])
        ntile = sb("ntile", [P, E])
        tend = sb("tend", [P, E])
        adj = sb("adj", [P, E])
        before = sb("before", [P, E])
        place = sb("place", [P, E, NT])
        pick = r_xg[:, 0:PAIRS * E].rearrange("p (c i e) -> p c i e", c=TOP_K, e=E)
        pos = sb("pos", [P, PAIRS])
        pos_i = sb("pos_i", [P, PAIRS], I32)
        hi_i = sb("hi_i", [P, PAIRS], I32)
        hi = sb("hi", [P, PAIRS], BF16)
        lo = sb("lo", [P, PAIRS], BF16)
        row_free = sb("row_free", [P, TILES])
        slot_row = sb("slot_row", [P, TILES], I32)
        cmp_t = r_interT[:, 0:TILES * E].rearrange("p (t e) -> p t e", e=E)
        eid = sb("eid", [P, TILES])
        eid_i = sb("eid_i", [P, TILES], I32)
        is_exp = sb("is_exp", [P, TILES, E])
        gidx = sb("gidx", [P, ROW_BUFS], I32)
        sidx = sb("sidx", [P, 2], I32)
        at_lane = region[:, ROW_BUFS * ROW:ROW_BUFS * ROW + PAIRS * P // 2].bitcast(BF16)\
            .rearrange("p (c l) -> p c l", l=P)
        placed = region[:, ROW_BUFS * ROW + 4 * D:ROW_BUFS * ROW + 6 * D + 4 * M].bitcast(BF16)
        at_tile = placed[:, 0:PAIRS * TILES].rearrange("p (c t) -> p c t", t=TILES)
        tile_val = placed[:, PAIRS * TILES:3 * PAIRS * TILES].rearrange("p (a c t) -> p a c t", a=2, t=TILES)
        wdump = sb("wdump", [P, 2, E])
        wslot = sb("wslot", [P, 2])

        ps_score, ps_mask = bank[0:2], bank[2:4]
        ps_cT, ps_q, ps_k = bank[4], bank[5], bank[4]
        ps_xT = bank[6]
        ps_logit, ps_last_logit = bank[7], bank[4]
        ps_within, ps_total, ps_slot = bank[0], bank[1], bank[4]
        ps_h, ps_gT, ps_iT, ps_y = bank[0:2], bank[2:4], bank[4:6], bank[6:8]

        s_wqk = sem("wqk_loaded")
        s_b = sem("biases_loaded")
        s_wg = sem("router_weights_loaded")
        s_gl = sem("gates_loaded")
        s_m8 = sem("mask_loaded")
        s_kp = sem("padding_mask_loaded")
        s_x = [sem(f"x_loaded_{i}") for i in range(B + 1)]
        s_c = [sem(f"ctx_loaded_{b}") for b in range(B)]
        s_wi = sem("wi_loaded")
        s_wo = sem("wo_loaded")
        s_hi = sem("wi_high_parts_made")
        s_split = sem("experts_split")
        s_const = sem("constants_made")
        s_bconst = sem("routing_constants_made")
        s_pool = sem("pool_step")
        s_tg = sem("gates_squashed")
        s_ms = sem("mask_addends_made")
        s_mb = sem("padding_addends_made")
        s_wT = sem("wqk_transposed")
        s_wTc = sem("wqk_copied")
        s_cT = sem("ctx_transposed")
        s_cTc = sem("ctx_copied")
        s_q = sem("q_projected")
        s_k = sem("k_projected")
        s_qc = sem("q_biased")
        s_kc = sem("k_biased")
        s_sc = sem("scores_and_mask_made")
        s_t1 = sem("scores_taken")
        s_t2 = sem("mask_taken")
        s_dve = sem("dve_step")
        s_aff = sem("exp_operands_ready")
        s_e = sem("exp_done")
        s_coef = sem("coefficients_ready")
        s_x1 = sem("x1_done_by_vector")
        s_x1p = sem("x1_done_by_pool")
        s_gs = sem("rsqrt_guessed")
        s_sh = sem("norm_operands_ready")
        s_cm = sem("router_means_made")
        s_wgc = sem("router_weights_centred")
        s_shv = sem("last_norm_operands_ready")
        s_xn = sem("xn_done")
        s_xT = sem("x1_transposed")
        s_xTc = sem("x1T_copied")
        s_lg = sem("logits_made")
        s_best = sem("top2_found")
        s_gap = sem("gap_ready")
        s_tgap = sem("gap_squashed")
        s_wt = sem("token_weights_ready")
        s_x1st = [sem(f"x1_stored_{b}") for b in range(B)]
        s_xnst = [sem(f"xn_stored_{b}") for b in range(B)]
        s_wst = sem("token_weights_stored")
        s_zst = sem("padding_stored")
        s_ch = sem("chosen_ready")
        s_rank = sem("ranks_made")
        s_lo = sem("slots_ready")
        s_at = sem("pair_tiles_placed")
        s_ln = sem("pair_lanes_placed")
        s_lane = sem("slot_lanes_ready")
        s_oh = sem("lane_onehots_ready")
        s_sl = sem("pair_summed")
        s_slot = sem("slot_rows_ready")
        s_eid = sem("tile_experts_ready")
        s_g = [sem(f"rows_gathered_{i}") for i in range(ROW_BUFS)]
        s_gT = sem("rows_transposed")
        s_gTc = sem("rowsT_high_made")
        s_gTl = sem("rowsT_low_made")
        s_h = sem("hidden_made")
        s_gate = sem("gate_done")
        s_ws = sem("slot_weight_ready")
        s_in = sem("inter_done")
        s_iT = sem("inter_transposed")
        s_iTc = sem("interT_copied")
        s_y = sem("y_made")
        s_yc = sem("y_copied")
        s_sct = sem("y_scattered")
        s_gi = sem("gather_index_ready")
        s_si = sem("scatter_index_ready")
        s_pass = sem("waits_passed")

        block = ctx.enter_context(nc.Block())

        out_v = out[0:tokens, :].rearrange("(b k p) d -> b p k d", b=B, p=P)
        xn_v = rows[0:tokens, 0:D].rearrange("(b k p) d -> b p k d", b=B, p=P)
        wt_v = rows[0:tokens, D:ROW].rearrange("(i p) e -> p i e", p=P)
        LAG = KT + 2
        NORM_GROUPS = [(KT * b, KT * (b + 1)) for b in range(B - 1)] + [(NT - KT, NT - 2)]

        def await_x1(eng, b, k):
            if k == KT - 1:
                eng.wait_ge(s_x1p, b + 1)
            else:
                eng.wait_ge(s_x1, (KT - 1) * b + k + 1)

        def split_low(eng, e, quarters=range(4)):
            assert DC == 4
            for c in quarters:
                if c == 0:
                    eng.wait_ge(s_hi, e + 1)
                if c == DC - 1 and e >= 1:
                    eng.wait_ge(s_split, e)
                ins = eng.tensor_tensor(wi_lo[:, e, c, :], wi_sb[:, e, c, :], wi_hi[:, e, c, :], ALU.subtract)
                if c == DC - 1:
                    ins.then_inc(s_split, 1)

        def tiles(t, b):
            return t[:, b * KT:(b + 1) * KT]

        @block.sync
        def _(sp):
            half = KT // 2
            x0 = x[0].rearrange("(k p) d -> p k d", p=P)
            sp.dma_start(wqk[:, 0, :], wq).then_inc(s_wqk, 16)
            for b in range(B):
                sp.dma_start(c_sb[:, b], ctx_in[b].rearrange("(k p) h -> p k h", p=P)).then_inc(s_c[b], 16)
                if b == 0:
                    for i in range(2):
                        sp.dma_start(x_sb[0][:, i * half:(i + 1) * half], x0[:, i * half:(i + 1) * half, :])\
                          .then_inc(s_x[i], 16)
                    sp.dma_start(m8[:, :, :], mask_st.rearrange("(k p) t -> p k t", p=P)).then_inc(s_m8, 16)
                else:
                    sp.dma_start(x_sb[b], x[b].rearrange("(k p) d -> p k d", p=P)).then_inc(s_x[b + 1], 16)
            for e in range(E):
                sp.dma_start(wi_sb[:, e, :, 0:M], wi_0[e].rearrange("(c p) m -> p c m", p=P)).then_inc(s_wi, 16)
                sp.dma_start(wi_sb[:, e, :, M:2 * M], wi_1[e].rearrange("(c p) m -> p c m", p=P)).then_inc(s_wi, 16)
            for e in range(E):
                sp.dma_start(wo_sb[:, e, :, :], wo[e].rearrange("(c p) d -> p c d", p=P)).then_inc(s_wo, 16)
            for b in range(B):
                await_x1(sp, b, KT - 2)
                await_x1(sp, b, KT - 1)
                sp.dma_start(out_v[b], x_sb[b]).then_inc(s_x1st[b], 16)
                sp.wait_ge(s_xn, KT * (b + 1))
                sp.dma_start(xn_v[b], prob[b % SOFT_BUFS]).then_inc(s_xnst[b], 16)

        @block.gpsimd
        def _(pool):
            step = [0]

            def link(ins):
                step[0] += 1
                ins.then_inc(s_pool, 1)
                pool.wait_ge(s_pool, step[0])

            def eye(t, pattern, fill=1.0, compare=ALU.not_equal):
                return pool.affine_select(out=t, in_=t, compare_op=compare, fill=fill, base=0, pattern=pattern,
                                          channel_multiplier=-1)

            pool.memset(batch_sel[:, :, :], 0.0)
            pool.memset(ident_h[:, :], 0.0)
            link(pool.memset(ident[:, :], 0.0))
            eye(ident[:, :], [[1, P]]).then_inc(s_const, 1)
            pool.memset(mean_of[:, :], 1.0 / D)
            eye(ident_h[:, :], [[1, P]])
            eye(batch_sel[:, :, :], [[1, B], [0, P]]).then_inc(s_const, 1)
            pool.dma_start(kp8[:, :], mask_bt).then_inc(s_kp, 16)
            pool.dma_start(gates[:, 0:1], g_attn.partition_broadcast(P)).then_inc(s_gl, 16)
            pool.dma_start(gates[:, 1:2], g_ffn.partition_broadcast(P)).then_inc(s_gl, 16)
            pool.iota(expert_m[:, :], [[1, E]], base=-E, channel_multiplier=0, allow_small_or_imprecise_dtypes=True)
            link(pool.memset(below[:, :], -1.0))
            pool.affine_select(out=below[:, :], in_=below[:, :], compare_op=ALU.is_ge, fill=0.0, base=0, pattern=[[-1, P]],
                               channel_multiplier=1)
            pool.memset(ones[:, :], 1.0)
            for t, pattern, base, mult in (
                (lane_row, [[1, P]], 0, 0), (tile_row, [[1, TILES]], 0, 0), (tile_from1, [[1, TILES]], 1, 0),
                (step_row, [[P, NT]], 0, 0), (pair_first, [[0, TOP_K], [P, NT]], -tokens, 0),
                (lane, [[0, 1]], 0, 1),
            ):
                pool.iota(t[:], pattern, base=base, channel_multiplier=mult, allow_small_or_imprecise_dtypes=True)
            link(pool.memset(zero_rows[:, :], 0.0))
            pool.dma_start(rows[tokens:tokens + P, :], zero_rows[:, :]).then_inc(s_zst, 16)
            pool.dma_start(out[tokens:tokens + P, :], zero_rows[:, 0:D]).then_inc(s_zst, 16)
            pool.memset(pos_i[:, :], 0).then_inc(s_bconst, 1)

            def newton(g):
                a, z = NORM_GROUPS[g]
                pool.wait_ge(s_gs, g + 1)
                v, y, t = veps[:, 1, a:z], guess[:, 1, a:z], tmp[:, 1, a:z]
                for n in range(3):
                    link(pool.tensor_tensor(t, y, y, ALU.mult))
                    link(pool.tensor_tensor(t, t, v, ALU.mult))
                    link(pool.tensor_scalar(t, t, -0.5, 1.5, ALU.mult, ALU.add))
                    link(pool.tensor_tensor(rstd[:, 1, a:z] if n == 2 else y, t, y, ALU.mult))
                link(pool.tensor_tensor(t, mv[:, 1, a:z, 0], rstd[:, 1, a:z], ALU.mult))
                pool.tensor_scalar(shift[:, a:z], t, -1.0, None, ALU.mult).then_inc(s_sh, 1)

            def residual(b):
                p, xs = prob[b % SOFT_BUFS][:, KT - 1, :], x_sb[b][:, KT - 1, :]
                pool.wait_ge(s_coef, b + 1)
                link(pool.tensor_scalar(p, p, coef[:, KT * (b + 1) - 1:KT * (b + 1)], None, ALU.mult))
                pool.tensor_tensor(xs, p, xs, ALU.add).then_inc(s_x1p, 1)

            residual(0)
            newton(0)
            residual(1)
            split_low(pool, 0)
            newton(1)
            residual(2)
            split_low(pool, 1)
            residual(3)
            newton(2)
            newton(3)
            split_low(pool, 3)

            full = [P, NT, E]
            pool.wait_ge(s_best, 2)
            pool.wait_ge(s_tgap, 1)
            for c, sign in enumerate((0.5, -0.5)):
                link(pool.tensor_scalar(share[:, c, :], tgap[:, :], sign, 0.5, ALU.mult, ALU.add))
                link(pool.tensor_scalar(share[:, c, :], share[:, c, :], tgates[:, 1:2], None, ALU.mult))
                link(pool.tensor_tensor(wparts[:, c], chose[:, c], share[:, c, :].unsqueeze(2).to_broadcast(full),
                                        ALU.mult))
            pool.tensor_tensor(wtok[:, :, :], wparts[:, 0], wparts[:, 1], ALU.add).then_inc(s_wt, 1)

            split_low(pool, 4, range(DC - 1))

            pt = [P, PAIRS, TILES]
            pool.wait_ge(s_lo, 1)
            pool.tensor_tensor(tile_val[:, 0], at_tile[:, :, :],
                               pair_first[:, :, :].rearrange("p c i -> p (c i)").unsqueeze(2).to_broadcast(pt),
                               ALU.mult).then_inc(s_at, 1)
            split_low(pool, 4, [DC - 1])

            pool.wait_ge(s_slot, 1)
            pool.wait_ge(s_zst, 32)
            pool.wait_ge(s_wst, 16)
            for b in range(B):
                pool.wait_ge(s_xnst[b], 16)
                pool.wait_ge(s_x1st[b], 16)

            def waited():
                pool.sem_inc(s_pass, 1)

            def gather(kk, r):
                q = r % ROW_BUFS
                pool.tensor_copy(gidx[:, q:q + 1], slot_row[:, bass.ds(ROW_BUFS * kk + r, 1)]).then_inc(s_gi, 1)
                pool.wait_ge(s_gi, ROW_BUFS * kk + r + 1)
                waited()
                pool.indirect_dma_start(xg[:, q, :], None, rows,
                                        bass.IndirectOffsetOnAxis(ap=gidx[:, q:q + 1], axis=0)).then_inc(s_g[q], 16)

            def scatter(kk, r):
                q = r % 2
                pool.tensor_copy(sidx[:, q:q + 1], slot_row[:, bass.ds(ROW_BUFS * kk + r, 1)]).then_inc(s_si, 1)
                pool.wait_ge(s_si, ROW_BUFS * kk + r + 1)
                pool.wait_ge(s_yc, ROW_BUFS * kk + r + 1)
                if r >= 1:
                    pool.wait_ge(s_sct, 16 * (ROW_BUFS * kk + r))
                waited()
                pool.indirect_dma_start(out, bass.IndirectOffsetOnAxis(ap=sidx[:, q:q + 1], axis=0), y_sb[:, q, :],
                                        None, compute_op=ALU.add).then_inc(s_sct, 16)

            for r in range(ROW_BUFS):
                gather(0, r)
            scatter(0, 0)
            gather(0, ROW_BUFS)
            turns = (TILES - ROW_BUFS - 1) // ROW_BUFS
            with pool.Fori(0, turns) as kk:
                for r in range(1, 1 + ROW_BUFS):
                    scatter(kk, r)
                    gather(kk, r + ROW_BUFS)
            for j in range(1 + turns * ROW_BUFS, TILES):
                scatter(0, j)
                if j + ROW_BUFS < TILES:
                    gather(0, j + ROW_BUFS)
            pool.wait_ge(s_sct, 16 * TILES)

        @block.scalar
        def _(act):
            act.dma_start(wqk[:, 1, :], wk).then_inc(s_wqk, 16)
            act.dma_start(bqk[:, 0:1], bq.rearrange("(o a) -> o a", a=1)).then_inc(s_b, 16)
            act.dma_start(bqk[:, 1:2], bk.rearrange("(o a) -> o a", a=1)).then_inc(s_b, 16)
            act.dma_start(wg_sb[:, :, :], w_gate.rearrange("(c p) e -> p c e", p=P)).then_inc(s_wg, 16)

            def project_out(b):
                act.wait_ge(s_cT, b + 1)
                if b >= 1:
                    act.wait_ge(s_k, b)
                act.activation(cT[:, :], ps_cT[:, :], ACT.Copy).then_inc(s_cTc, 1)
                if b == 0:
                    act.wait_ge(s_kp, 16)
                    act.activation(mask_b[:, :], kp8[:, :], ACT.Copy, scale=MASKED).then_inc(s_mb, 1)
                    act.wait_ge(s_m8, 16)
                    for k in range(KT):
                        act.activation(mask_s[:, k, :], m8[:, k, :], ACT.Copy, scale=MASKED).then_inc(s_ms, 1)
                    act.wait_ge(s_b, 32)
                if b >= 2:
                    act.wait_ge(s_sc, KT * (b - 1))
                act.wait_ge(s_q, b + 1)
                act.activation(qkT[:, b % 2, 0, :], ps_q[:, :], ACT.Identity, bias=bqk[:, 0:1]).then_inc(s_qc, 1)
                act.wait_ge(s_k, b + 1)
                act.activation(qkT[:, b % 2, 1, :], ps_k[:, :], ACT.Identity, bias=bqk[:, 1:2]).then_inc(s_kc, 1)

            def exp(b, k):
                i = KT * b + k
                act.wait_ge(s_aff, i + 1)
                act.activation(prob[b % SOFT_BUFS][:, k, :], prob[b % SOFT_BUFS][:, k, :], ACT.Exp, scale=esc[:, i:i + 1],
                               bias=ebi[:, i:i + 1], accum_out=esum[:, i:i + 1]).then_inc(s_e, 1)

            def norm(i):
                b, k = i // KT, i % KT
                if i == NT - 2:
                    act.wait_ge(s_shv, 1)
                elif k == 0:
                    act.wait_ge(s_sh, b + 1)
                act.activation(prob[b % SOFT_BUFS][:, k, :], x_sb[b][:, k, :], ACT.Identity,
                               scale=rstd[:, 1, i:i + 1], bias=shift[:, i:i + 1]).then_inc(s_xn, 1)

            def split_hi(e, half):
                if e == 0 and half == 0:
                    act.wait_ge(s_wi, 16 * 2 * E)
                    act.wait_ge(s_cT, B)
                if e in X_AT and half == 0:
                    b = X_AT.index(e)
                    act.wait_ge(s_x1st[b], 16)
                    act.wait_ge(s_xT, KT * (b + 1))
                    act.wait_ge(s_gs, b + 1)
                    act.wait_ge(s_xn, KT * (b + 1))
                    if b == B - 1:
                        act.wait_ge(s_shv, 1)
                if e in PROB_AT and half == 0:
                    b = max(b for b in range(B) if b % SOFT_BUFS == PROB_AT.index(e))
                    act.wait_ge(s_xnst[b], 16)
                for c in range(half * DC // 2, (half + 1) * DC // 2):
                    last = act.activation(wi_hi[:, e, c, :], wi_sb[:, e, c, :], ACT.Copy)
                if half == 1:
                    last.then_inc(s_hi, 1)

            def turned(i):
                act.wait_ge(s_xT, i + 1)
                if i >= 2:
                    act.wait_ge(s_lg, i - 1)
                act.activation(x1T[:, i % 2].rearrange("p c t -> p (c t)"), ps_xT[:, :], ACT.Copy).then_inc(s_xTc, 1)

            act.wait_ge(s_wT, 1)
            act.activation(wqkT[:, :, :].rearrange("p a o -> p (a o)"), ps_xT[:, 0:2 * P], ACT.Copy).then_inc(s_wTc, 1)
            project_out(0)
            act.wait_ge(s_gl, 32)
            act.activation(tgates[:, :], gates[:, :], ACT.Tanh).then_inc(s_tg, 1)
            for b in range(B - 1):
                project_out(b + 1)
                for k in range(KT):
                    i = KT * b + k
                    exp(b, k)
                    if i >= LAG:
                        turned(i - LAG)
                    if b == B - 2 and k < 2:
                        split_hi(0, k)
                    if b == B - 2 and k in (1, 2):
                        norm(2 * (k - 1))
                        norm(2 * (k - 1) + 1)
            turned(NT - 10)
            turned(NT - 9)
            turned(NT - 8)
            exp(B - 1, 0)
            split_hi(1, 0)
            turned(NT - 7)
            split_hi(1, 1)
            exp(B - 1, 1)
            norm(KT)
            turned(NT - 6)
            exp(B - 1, 2)
            turned(NT - 5)
            exp(B - 1, 3)
            for i in range(KT + 1, 2 * KT):
                norm(i)
            split_hi(2, 0)
            split_hi(2, 1)
            turned(NT - 4)
            split_hi(3, 0)
            turned(NT - 3)
            split_hi(3, 1)
            turned(NT - 2)
            turned(NT - 1)
            for i in range(2 * KT, NT):
                norm(i)
            act.wait_ge(s_gap, 1)
            act.activation(tgap[:, :], gap[:, :], ACT.Tanh, scale=0.5).then_inc(s_tgap, 1)
            split_hi(4, 0)
            split_hi(4, 1)
            split_hi(5, 0)
            split_hi(5, 1)
            act.wait_ge(s_lo, 1)
            act.activation(tile_val[:, 1], at_tile[:, :, :], ACT.Copy, scale=lane[:, 0:1]).then_inc(s_ln, 1)
            for e in range(6, E):
                split_hi(e, 0)
                split_hi(e, 1)
            act.wait_ge(s_tgap, 1)
            act.activation(table_trial[:, :], tgap[:, 0:1], ACT.Silu)
            act.wait_ge(s_wt, 1)
            act.dma_start(wt_v, wtok[:, :, :]).then_inc(s_wst, 16)

            def rows_out(kk, r):
                j = ROW_BUFS * kk + r
                act.wait_ge(s_gT, j + 1)
                if r >= 2:
                    act.wait_ge(s_h, j - 1)
                act.activation(xgT_hi[:, r % 2, :], ps_gT[r % 2][:, :], ACT.Copy).then_inc(s_gTc, 1)

            def silu(kk, r):
                j = ROW_BUFS * kk + r
                act.wait_ge(s_h, j + 1)
                if r >= 2:
                    act.wait_ge(s_in, j - 1)
                act.activation(gate[:, r % 2, :], ps_h[r % 2][:, 0:M], ACT.Silu).then_inc(s_gate, 1)

            rows_out(0, 0)
            rows_out(0, 1)
            silu(0, 0)
            silu(0, 1)
            with act.Fori(0, LOOPS) as kk:
                for r in range(2, 2 + ROW_BUFS):
                    rows_out(kk, r)
                    silu(kk, r)
            rows_out(0, TILES - 1)
            silu(0, TILES - 1)

        @block.tensor
        def _(pe):
            pe.wait_ge(s_wqk, 32)
            pe.wait_ge(s_const, 1)
            for i in range(2):
                last = pe.transpose(ps_xT[:, i * P:(i + 1) * P], wqk[:, i, :], ident[:, :])
            last.then_inc(s_wT, 1)
            def project(b):
                pe.wait_ge(s_c[b], 16)
                if b >= 1:
                    pe.wait_ge(s_kc, b)
                for k in range(KT):
                    last = pe.transpose(ps_cT[:, k * P:(k + 1) * P], c_sb[:, b, k, :], ident[:, :])
                last.then_inc(s_cT, 1)
                pe.wait_ge(s_cTc, b + 1)
                if b == 0:
                    pe.wait_ge(s_wTc, 1)
                if b >= 1:
                    pe.wait_ge(s_qc, b)
                pe.matmul(ps_q[:, :], wqkT[:, 0, :], cT[:, :], start=True, stop=True).then_inc(s_q, 1)
                pe.matmul(ps_k[:, :], wqkT[:, 1, :], cT[:, :], start=True, stop=True).then_inc(s_k, 1)

            def score(i):
                b, k = i // KT, i % KT
                if k == 0:
                    pe.wait_ge(s_qc, b + 1)
                    pe.wait_ge(s_kc, b + 1)
                if i >= 2:
                    pe.wait_ge(s_t1, i - 1)
                pe.matmul(ps_score[i % 2][:, :], qkT[:, b % 2, 0, k * P:(k + 1) * P], qkT[:, b % 2, 1, :],
                          start=True, stop=True)
                if i == 0:
                    pe.wait_ge(s_const, 2)
                    pe.wait_ge(s_mb, 1)
                if i < KT:
                    pe.wait_ge(s_ms, i + 1)
                if i >= 2:
                    pe.wait_ge(s_t2, i - 1)
                pe.matmul(ps_mask[i % 2][:, :], ident_h[:, :], mask_s[:, k, :], start=True, stop=False)
                pe.matmul(ps_mask[i % 2][:, :], batch_sel[:, b, :], mask_b[:, :], start=False, stop=True)\
                  .then_inc(s_sc, 1)

            def turn(i):
                b, k = i // KT, i % KT
                await_x1(pe, b, k)
                if i >= 1:
                    pe.wait_ge(s_xTc, i)
                else:
                    pe.wait_ge(s_wTc, 1)
                for c in range(DC):
                    last = pe.transpose(ps_xT[:, c * P:(c + 1) * P], x_sb[b][:, k, c * P:(c + 1) * P], ident[:, :])
                last.then_inc(s_xT, 1)

            def route(i):
                pe.wait_ge(s_xTc, i + 1)
                if i == 0:
                    pe.wait_ge(s_wgc, 1)
                for c in range(DC):
                    last = pe.matmul((ps_logit if i < NT - KT else ps_last_logit)[:, i * E:(i + 1) * E], x1T[:, i % 2, c, :], wgc[:, c, :],
                                     start=(c == 0), stop=(c == DC - 1))
                last.then_inc(s_lg, 1)

            project(0)
            score(0)
            score(1)
            pe.wait_ge(s_wg, 16)
            pe.wait_ge(s_const, 2)
            for c in range(DC):
                last = pe.matmul(ps_logit[:, 0:E], mean_of[:, :], wg_sb[:, c, :], start=(c == 0), stop=(c == DC - 1))
            last.then_inc(s_cm, 1)
            for b in range(B - 1):
                project(b + 1)
                for k in range(KT):
                    i = KT * b + k
                    score(i + 2)
                    if i >= LAG:
                        turn(i - LAG)
                    if i > LAG:
                        route(i - LAG - 1)
            for i in range(NT - KT - LAG, NT):
                if i == NT - LAG - 1:
                    score(NT - 2)
                if i == NT - LAG:
                    score(NT - 1)
                turn(i)
                route(i - 1)
            route(NT - 1)

            pe.wait_ge(s_bconst, 1)
            pe.wait_ge(s_ch, 1)
            ch = chosen[:, :, :].rearrange("p e i -> p (e i)")
            pe.matmul(ps_total[:, 0:E * NT], ones[:, :], ch, start=True, stop=True)
            pe.matmul(ps_within[:, 0:E * NT], below[:, :], ch, start=True, stop=True).then_inc(s_rank, 1)
            pe.wait_ge(s_at, 1)
            pe.wait_ge(s_ln, 1)
            for j in range(PAIRS):
                if j % 8 == 0:
                    pe.wait_ge(s_oh, j // 8 + 1)
                for a in range(2):
                    last = pe.matmul(ps_slot[:, 0:TILES], at_lane[:, j, :], tile_val[:, a, j, :],
                                     start=(j + a == 0), stop=(j + a == PAIRS))
            last.then_inc(s_sl, 1)

            def rows_turn(kk, r):
                j = ROW_BUFS * kk + r
                pe.wait_ge(s_g[r % ROW_BUFS], 16 * (kk + r // ROW_BUFS + 1))
                if r >= 2:
                    pe.wait_ge(s_gTl, j - 1)
                for c in range(DC):
                    last = pe.transpose(ps_gT[r % 2][:, c * P:(c + 1) * P],
                                        xg[:, r % ROW_BUFS, c * P:(c + 1) * P], ident[:, :])
                last.then_inc(s_gT, 1)

            def expert(kk, r):
                return pe.value_load(eid_i[0:1, bass.ds(ROW_BUFS * kk + r, 1)], min_val=0, max_val=E - 1)

            def hidden(kk, r, e):
                j = ROW_BUFS * kk + r
                pe.wait_ge(s_gTl, j + 1)
                if r >= 2:
                    pe.wait_ge(s_in, j - 1)
                pe.wait_ge(s_split, e + 1)
                for n, (xs, ws) in enumerate(((xgT_hi, wi_hi), (xgT_hi, wi_lo), (xgT_lo, wi_hi))):
                    for c in range(DC):
                        last = pe.matmul(ps_h[r % 2][:, :], xs[:, r % 2, c * P:(c + 1) * P], ws[:, bass.ds(e, 1), c, :],
                                         start=(n + c == 0), stop=(n == 2 and c == DC - 1))
                last.then_inc(s_h, 1)

            def inter_turn(kk, r):
                j = ROW_BUFS * kk + r
                pe.wait_ge(s_in, j + 1)
                if r >= 2:
                    pe.wait_ge(s_iTc, j - 1)
                for c in range(MC):
                    last = pe.transpose(ps_iT[r % 2][:, c * P:(c + 1) * P], inter[:, r % 2, c * P:(c + 1) * P],
                                        ident[:, :])
                last.then_inc(s_iT, 1)

            def down(kk, r, e):
                j = ROW_BUFS * kk + r
                pe.wait_ge(s_iTc, j + 1)
                if r >= 2:
                    pe.wait_ge(s_yc, j - 1)
                for c in range(MC):
                    last = pe.matmul(ps_y[r % 2][:, :], interT[:, r % 2, c * P:(c + 1) * P],
                                     wo_sb[:, bass.ds(e, 1), c, :], start=(c == 0), stop=(c == MC - 1))
                last.then_inc(s_y, 1)

            def keep_warm(times):
                for i in range(times):
                    pe.matmul(ps_y[0][:, :], ident_h[:, :], at_lane[:, 0:4, :].rearrange("p c l -> p (c l)"),
                              start=True, stop=True)

            keep_warm(20)
            pe.wait_ge(s_wo, 16 * E)
            pe.wait_ge(s_eid, 1)
            rows_turn(0, 0)
            rows_turn(0, 1)
            first, second = expert(0, 0), expert(0, 1)
            hidden(0, 0, first)
            hidden(0, 1, second)
            inter_turn(0, 0)
            rows_turn(0, 2)
            down(0, 0, first)
            inter_turn(0, 1)

            def step_tile(kk, r, before, this, last_of_turn=False, end=False):
                hidden(kk, r, this)
                if not end:
                    rows_turn(kk, r + 1)
                if before is None:
                    before = expert(kk, r - 1)
                following = None if last_of_turn or end else expert(kk, r + 1)
                down(kk, r - 1, before)
                inter_turn(kk, r)
                return this, following

            with pe.Fori(0, LOOPS // PE_TURNS) as kk:
                this = expert(PE_TURNS * kk, 2)
                before = None
                for r in range(2, 2 + PE_TURNS * ROW_BUFS):
                    before, this = step_tile(PE_TURNS * kk, r, before, this, last_of_turn=r == 1 + PE_TURNS * ROW_BUFS)
            this = expert(0, TILES - 1)
            step_tile(0, TILES - 1, None, this, end=True)
            down(0, TILES - 1, this)

        @block.vector
        def _(dve):
            steps = [0]

            def link(ins):
                steps[0] += 1
                ins.then_inc(s_dve, 1)
                dve.wait_ge(s_dve, steps[0])

            def bcast(ap, shape):
                return ap.to_broadcast(shape)

            def statistics(norm, i):
                link(dve.bn_stats(stats[:, i % 8, :], x_sb[i // KT][:, i % KT, :]))
                return dve.bn_aggr(mv[:, norm, i, :], stats[:, i % 8, :])

            def guessed(norm, a, z):
                v, y = veps[:, norm, a:z], guess[:, norm, a:z]
                link(dve.tensor_scalar(v, mv[:, norm, a:z, 1], EPS, None, ALU.add))
                link(dve.tensor_scalar(y.bitcast(I32), v.bitcast(I32), 1, None, ALU.arith_shift_right))
                return dve.tensor_scalar(y.bitcast(I32), y.bitcast(I32), -1.0, float(RSQRT_MAGIC), ALU.mult, ALU.add)

            def newton(norm, a, z):
                v, y, t = veps[:, norm, a:z], guess[:, norm, a:z], tmp[:, norm, a:z]
                for n in range(3):
                    link(dve.tensor_tensor(t, y, y, ALU.mult))
                    link(dve.scalar_tensor_tensor(out=t, in0=t, scalar=-0.5, in1=v, op0=ALU.mult, op1=ALU.mult))
                    link(dve.scalar_tensor_tensor(out=rstd[:, norm, a:z] if n == 2 else y, in0=t, scalar=1.5, in1=y,
                                                  op0=ALU.add, op1=ALU.mult))

            def first_rstd(a, z):
                link(guessed(0, a, z))
                newton(0, a, z)
                link(dve.tensor_scalar(esc[:, a:z], rstd[:, 0, a:z], scale, None, ALU.mult))

            def first_stats(i):
                b, k = i // KT, i % KT
                if b > 0 and k == 0:
                    dve.wait_ge(s_x[b + 1], 16)
                elif b == 0 and k % (KT // 2) == 0:
                    dve.wait_ge(s_x[k // (KT // 2)], 16)
                return statistics(0, i)

            def attend(b, k):
                i = KT * b + k
                dve.wait_ge(s_sc, i + 1)
                s = prob[b % SOFT_BUFS][:, k, :]
                if b >= SOFT_BUFS and k == 0:
                    dve.wait_ge(s_xnst[b - SOFT_BUFS], 16)
                dve.scalar_tensor_tensor(out=s, in0=x_sb[b][:, k, :], scalar=mv[:, 0, i, 0:1],
                                         in1=ps_score[i % 2][:, :], op0=ALU.subtract,
                                         op1=ALU.mult).then_inc(s_t1, 1)
                dve.wait_ge(s_t1, i + 1)
                dve.tensor_tensor_reduce(s, s, ps_mask[i % 2][:, :], 1.0, -3e38, ALU.add, ALU.max,
                                         smax[:, i:i + 1]).then_inc(s_t2, 1)
                dve.wait_ge(s_t2, i + 1)
                dve.scalar_tensor_tensor(out=ebi[:, i:i + 1], in0=smax[:, i:i + 1], scalar=-1.0,
                                         in1=esc[:, i:i + 1], op0=ALU.mult, op1=ALU.mult).then_inc(s_aff, 1)

            def coefficients(b):
                lv, cf = tiles(live, b), tiles(coef, b)
                link(dve.tensor_scalar(lv, tiles(smax, b), ALL_MASKED, None, ALU.is_gt))
                dve.wait_ge(s_e, KT * (b + 1))
                link(dve.tensor_tensor(cf, tiles(esum, b), lv, ALU.mult))
                link(dve.reciprocal(cf, cf))
                if b == 0:
                    dve.wait_ge(s_tg, 1)
                dve.scalar_tensor_tensor(out=cf, in0=cf, scalar=tgates[:, 0:1], in1=lv, op0=ALU.mult,
                                         op1=ALU.mult).then_inc(s_coef, 1)
                dve.wait_ge(s_coef, b + 1)

            def residual(b, k):
                i = KT * b + k
                if k < KT - 1:
                    dve.scalar_tensor_tensor(out=x_sb[b][:, k, :], in0=prob[b % SOFT_BUFS][:, k, :],
                                             scalar=coef[:, i:i + 1], in1=x_sb[b][:, k, :], op0=ALU.mult,
                                             op1=ALU.add).then_inc(s_x1, 1)
                await_x1(dve, b, k)
                return statistics(1, i)

            for i in range(KT):
                last = first_stats(i)
            link(last)
            first_rstd(0, KT)
            for k in range(KT):
                attend(0, k)
                for i in range(KT + (B - 1) * k, KT + (B - 1) * (k + 1)):
                    last = first_stats(i)
            link(last)
            first_rstd(KT, NT)
            dve.wait_ge(s_cm, 1)
            dve.tensor_tensor(wgc[:, :, :], wg_sb[:, :, :], bcast(ps_logit[:, 0:E].unsqueeze(1), [P, DC, E]),
                              ALU.subtract).then_inc(s_wgc, 1)
            for b in range(1, B):
                if b == SOFT_BUFS:
                    coefficients(b - 1)
                    residual(b - 1, 0)
                for k in range(KT):
                    attend(b, k)
                    if b < SOFT_BUFS and k == 0:
                        coefficients(b - 1)
                    elif b < SOFT_BUFS:
                        residual(b - 1, k - 1)
                    elif k < KT - 2:
                        residual(b - 1, k + 1)
                link(residual(b - 1, KT - 1))
                guessed(1, KT * (b - 1), KT * b).then_inc(s_gs, 1)
            coefficients(B - 1)
            residual(B - 1, 0)
            link(residual(B - 1, 1))
            guessed(1, NT - KT, NT - 2).then_inc(s_gs, 1)
            residual(B - 1, 2)
            link(residual(B - 1, 3))
            link(guessed(1, NT - 2, NT))
            newton(1, NT - 2, NT)
            dve.scalar_tensor_tensor(out=shift[:, NT - 2:NT], in0=mv[:, 1, NT - 2:NT, 0], scalar=-1.0,
                                     in1=rstd[:, 1, NT - 2:NT], op0=ALU.mult, op1=ALU.mult).then_inc(s_shv, 1)

            def top2(a, z, ps):
                full = [P, z - a, E]
                em = bcast(expert_m[:, :].unsqueeze(1), full)
                lg, ca = logit[:, a:z, :], cand[:, a:z, :]
                link(dve.tensor_tensor(lg, ps[:, a * E:z * E].rearrange("p (i e) -> p i e", e=E),
                                       bcast(rstd[:, 1, a:z].unsqueeze(2), full), ALU.mult))
                for c in range(TOP_K):
                    one = chose[:, c, a:z, :]
                    link(dve.tensor_reduce(best[:, c, a:z], lg, AX_X, ALU.max))
                    link(dve.tensor_tensor(ca, lg, bcast(best[:, c, a:z].unsqueeze(2), full), ALU.is_equal))
                    link(dve.tensor_tensor(ca, ca, em, ALU.mult))
                    link(dve.tensor_reduce(which[:, a:z], ca, AX_X, ALU.min))
                    ins = dve.tensor_tensor(one, em, bcast(which[:, a:z].unsqueeze(2), full), ALU.is_equal)
                    if c == 0:
                        link(ins)
                        link(dve.scalar_tensor_tensor(out=lg, in0=one, scalar=-1e38, in1=lg, op0=ALU.mult,
                                                      op1=ALU.add))
                    else:
                        ins.then_inc(s_best, 1)

            split_low(dve, 2)
            dve.wait_ge(s_bconst, 1)
            dve.wait_ge(s_sh, B - 1)
            dve.wait_ge(s_lg, NT - KT)
            top2(0, NT - KT, ps_logit)
            dve.wait_ge(s_sh, B)
            dve.wait_ge(s_shv, 1)
            dve.wait_ge(s_lg, NT)
            top2(NT - KT, NT, ps_last_logit)
            dve.wait_ge(s_best, 2)
            dve.tensor_tensor(gap[:, :], best[:, 0, :], best[:, 1, :], ALU.subtract).then_inc(s_gap, 1)

            dve.tensor_tensor(chosen[:, :, :], chose[:, 0].rearrange("p i e -> p e i"),
                              chose[:, 1].rearrange("p i e -> p e i"), ALU.add).then_inc(s_ch, 1)
            dve.wait_ge(s_rank, 1)
            flat = lambda t: t[:, :, :].rearrange("p e i -> p (e i)")
            en = [P, E, NT]
            link(dve.tensor_copy(flat(total), ps_total[:, 0:E * NT]))
            link(dve.tensor_tensor_scan(incl[:, :], flat(total), flat(total), 0.0, ALU.add, ALU.bypass))
            link(dve.tensor_reduce(count[:, :], total[:, :, :], AX_X, ALU.add))
            last_incl = incl[:, :].rearrange("p (e i) -> p e i", e=E)[:, :, NT - 1]
            dve.scalar_tensor_tensor(out=before[:, :], in0=count[:, :], scalar=float(P), in1=last_incl,
                                     op0=ALU.add, op1=ALU.subtract)
            dve.tensor_tensor(flat(place), incl[:, :], ps_within[:, 0:E * NT], ALU.add)
            link(dve.tensor_tensor(cmp_c[:, :, :], bcast(count[:, :].unsqueeze(2), en),
                                   bcast(step_row[:, :].unsqueeze(1), en), ALU.is_gt))
            link(dve.tensor_reduce(ntile[:, :], cmp_c[:, :, :], AX_X, ALU.add))
            dve.scalar_tensor_tensor(out=adj[:, :], in0=ntile[:, :], scalar=-float(P), in1=before[:, :],
                                     op0=ALU.mult, op1=ALU.add)
            link(dve.tensor_tensor_scan(tend[:, :], ntile[:, :], ntile[:, :], 0.0, ALU.add, ALU.bypass))
            link(dve.scalar_tensor_tensor(out=adj[:, :], in0=tend[:, :], scalar=float(P), in1=adj[:, :],
                                          op0=ALU.mult, op1=ALU.add))
            link(dve.tensor_tensor(place[:, :, :], place[:, :, :], bcast(adj[:, :].unsqueeze(2), en), ALU.add))
            for c in range(TOP_K):
                ins = dve.tensor_tensor(pick[:, c], chose[:, c], place[:, :, :].rearrange("p e i -> p i e"), ALU.mult)
            link(ins)
            link(dve.tensor_reduce(pos[:, :], pick[:, :, :, :].rearrange("p c i e -> p (c i) e"), AX_X, ALU.add))
            link(dve.tensor_copy(pos_i[:, :], pos[:, :]))
            link(dve.tensor_scalar(hi_i[:, :], pos_i[:, :], 7, None, ALU.arith_shift_right))
            link(dve.tensor_copy(hi[:, :], hi_i[:, :]))
            dve.scalar_tensor_tensor(out=lo[:, :], in0=hi[:, :], scalar=-float(P), in1=pos[:, :],
                                     op0=ALU.mult, op1=ALU.add).then_inc(s_lane, 1)
            pt, pl = [P, PAIRS, TILES], [P, 8, P]
            dve.wait_ge(s_zst, 32)
            dve.tensor_tensor(at_tile[:, :, :], bcast(tile_from1[:, :].unsqueeze(1), pt),
                              bcast(hi[:, :].unsqueeze(2), pt), ALU.is_equal).then_inc(s_lo, 1)
            dve.wait_ge(s_lane, 1)
            for a in range(0, PAIRS, 8):
                dve.tensor_tensor(at_lane[:, a:a + 8, :], bcast(lane_row[:, :].unsqueeze(1), pl),
                                  bcast(lo[:, a:a + 8].unsqueeze(2), pl), ALU.is_equal).then_inc(s_oh, 1)
            te = [P, TILES, E]
            link(dve.tensor_tensor(cmp_t[:, :, :], bcast(tile_row[:, :].unsqueeze(2), te),
                                   bcast(tend[:, :].unsqueeze(1), te), ALU.is_ge))
            link(dve.tensor_reduce(eid[:, :], cmp_t[:, :, :], AX_X, ALU.add))
            link(dve.tensor_scalar(eid[:, :], eid[:, :], float(E - 1), None, ALU.min))
            dve.wait_ge(s_sl, 1)
            link(dve.tensor_scalar(row_free[:, :], ps_slot[:, 0:TILES], 0.0, lane[:, 0:1], ALU.is_equal, ALU.mult))
            dve.scalar_tensor_tensor(out=slot_row[:, :], in0=ps_slot[:, 0:TILES], scalar=float(tokens),
                                     in1=row_free[:, :], op0=ALU.add, op1=ALU.add).then_inc(s_slot, 1)
            dve.tensor_copy(eid_i[:, :], eid[:, :]).then_inc(s_eid, 1)
            link(dve.tensor_scalar(eid[:, :], eid[:, :], -float(E), None, ALU.add))
            link(dve.tensor_tensor(is_exp[:, :, :], bcast(expert_m[:, :].unsqueeze(1), te),
                                   bcast(eid[:, :].unsqueeze(2), te), ALU.is_equal))

            split_low(dve, 5)

            def slot_weight(kk, r):
                j = ROW_BUFS * kk + r
                q = r % ROW_BUFS
                dve.wait_ge(s_g[q], 16 * (kk + r // ROW_BUFS + 1))
                dve.scalar_tensor_tensor(out=wdump[:, r % 2, :], in0=xg[:, q, D:ROW], scalar=1.0,
                                         in1=is_exp[:, bass.ds(j, 1), :].rearrange("p a e -> p (a e)"),
                                         op0=ALU.mult, op1=ALU.mult,
                                         accum_out=wslot[:, r % 2:r % 2 + 1]).then_inc(s_ws, 1)

            def rows_lo(kk, r):
                j = ROW_BUFS * kk + r
                dve.wait_ge(s_gTc, j + 1)
                if r >= 2:
                    dve.wait_ge(s_h, j - 1)
                dve.tensor_tensor(xgT_lo[:, r % 2, :], ps_gT[r % 2][:, :], xgT_hi[:, r % 2, :],
                                  ALU.subtract).then_inc(s_gTl, 1)

            def combine(kk, r):
                j = ROW_BUFS * kk + r
                dve.wait_ge(s_ws, j + 1)
                dve.wait_ge(s_gate, j + 1)
                if r >= 2:
                    dve.wait_ge(s_iT, j - 1)
                dve.scalar_tensor_tensor(out=inter[:, r % 2, :], in0=gate[:, r % 2, :], scalar=wslot[:, r % 2:r % 2 + 1],
                                         in1=ps_h[r % 2][:, M:2 * M], op0=ALU.mult, op1=ALU.mult).then_inc(s_in, 1)

            def inter_out(kk, r):
                j = ROW_BUFS * kk + r
                dve.wait_ge(s_iT, j + 1)
                if r >= 2:
                    dve.wait_ge(s_y, j - 1)
                dve.tensor_copy(interT[:, r % 2, :], ps_iT[r % 2][:, 0:M]).then_inc(s_iTc, 1)

            def y_out(kk, r):
                j = ROW_BUFS * kk + r
                dve.wait_ge(s_y, j + 1)
                if r >= 2:
                    dve.wait_ge(s_sct, 16 * (j - 1))
                dve.tensor_copy(y_sb[:, r % 2, :], ps_y[r % 2][:, :]).then_inc(s_yc, 1)

            def step_tile(kk, r, last=False):
                slot_weight(kk, r)
                combine(kk, r)
                if not last:
                    rows_lo(kk, r + 1)
                y_out(kk, r - 1)
                inter_out(kk, r)

            split_low(dve, 6)
            rows_lo(0, 0)
            rows_lo(0, 1)
            slot_weight(0, 0)
            split_low(dve, 7)
            combine(0, 0)
            inter_out(0, 0)
            step_tile(0, 1)
            with dve.Fori(0, LOOPS) as kk:
                for r in range(2, 2 + ROW_BUFS):
                    step_tile(kk, r)
            step_tile(0, TILES - 1, last=True)
            y_out(0, TILES - 1)


_INS = ['x', 'ctx_512', 'mask_SxS2_bk1', 'mask_BxS2_bf0', 'g_xattn', 'g_ffn', 'L0_xattn_Wq', 'L0_xattn_bq',
        'L0_xattn_Wk', 'L0_xattn_bk', 'L0_ffn_w_gate', 'L0_ffn_wi_0', 'L0_ffn_wi_1', 'L0_ffn_wo']


def kernel(**inputs):
    import numpy as _np
    import concourse.bacc as _bacc
    from concourse import mybir as _mybir
    from concourse.bass_utils import run_bass_kernel_spmd as _run

    nc = _bacc.Bacc("TRN2", target_bir_lowering=False, num_devices=1)
    arrays, args = {}, []
    for name in _INS:
        a = _np.ascontiguousarray(inputs[name])
        arrays[f"in_{name}_dram"] = a
        args.append(nc.dram_tensor(f"in_{name}_dram", a.shape, _mybir.dt.from_np(a.dtype), kind="ExternalInput").ap())
    B, S, D = inputs['x'].shape
    E = inputs['L0_ffn_w_gate'].shape[1]
    out = nc.dram_tensor("out_0_dram", (B * S + P, D), F32, kind="ExternalOutput").ap()
    rows = nc.dram_tensor("normed_rows", (B * S + P, D + E), F32, kind="Internal").ap()
    gated_attention_moe(nc, *args, out, rows)
    r = _run(nc, [arrays], core_ids=[0])
    return r.results[0]["out_0_dram"][:B * S].reshape(B, S, D)
```
